# Optimizing a Trainium2 kernel written in Bass

```python
import numpy as np
import jax
import jax.numpy as jnp

def _softmax(x, axis=-1):
    return jax.nn.softmax(x, axis=axis)

def _gelu(x):
    return jax.nn.gelu(x, approximate=True)

def _silu(x):
    return jax.nn.silu(x)

def _sigmoid(x):
    return jax.nn.sigmoid(x)

def _layernorm(x, axis=-1, eps=1e-05):
    m = jnp.mean(x, axis=axis, keepdims=True)
    v = jnp.var(x, axis=axis, keepdims=True)
    return (x - m) / jnp.sqrt(v + eps)

def _scatter_add(tgt, idx, src, axis=0):
    return tgt.at[idx].add(src)

def _segment_sum(src, seg, n):
    return jax.ops.segment_sum(src, seg, n)
kernel_name = 'mk_gnn_resnorm_d4_gnn_r8_c5eed4'

def setup_inputs(seed: int=0):
    np.random.seed(seed)
    _w = jnp.asarray

    def _rec_inputs():
        import jax
        import jax.numpy as jnp
        _gk = jax.random.key(seed)
        x = -8.776e-05 + 1 * jax.random.normal(jax.random.fold_in(_gk, 1), (6250, 256), jnp.float32)
        src = jax.random.randint(jax.random.fold_in(_gk, 2), (100000,), 0, 6250, jnp.int32)
        dst = jax.random.randint(jax.random.fold_in(_gk, 3), (100000,), 0, 6250, jnp.int32)
        _o = jnp.argsort(dst, stable=True)
        src = src[_o]
        dst = dst[_o]
        edge_attr_3 = -1.09012e-05 + 0.99985 * jax.random.normal(jax.random.fold_in(_gk, 12), (100000, 3), jnp.float32)
        edge_type_16 = jax.random.randint(jax.random.fold_in(_gk, 14), (100000,), 0, 16, jnp.int32)
        edge_type_20 = jax.random.randint(jax.random.fold_in(_gk, 15), (100000,), 0, 20, jnp.int32)
        edge_type_32 = jax.random.randint(jax.random.fold_in(_gk, 16), (100000,), 0, 32, jnp.int32)
        edge_weight1 = jax.random.uniform(jax.random.fold_in(_gk, 17), (100000, 1), jnp.float32, 0.0, 0.999998)
        return (x, src, dst, edge_attr_3, edge_type_16, edge_type_20, edge_type_32, edge_weight1)
    x, src, dst, edge_attr_3, edge_type_16, edge_type_20, edge_type_32, edge_weight1 = _rec_inputs()

    def _L0_gnn_setup():
        import jax, jax.numpy as jnp
        import numpy as np
        N_NODES = 2500
        N_EDGES = 40000
        IN_DIM = 256
        OUT_DIM = 256
        NUM_RELS = 32
        NUM_BASES = 8
        key = jax.random.key(seed)
        k1, k2, k3, k4, k5, k6, k7 = jax.random.split(key, 7)
        h = jax.random.normal(k1, (N_NODES, IN_DIM), dtype=jnp.float32)
        src = jax.random.randint(k2, (N_EDGES,), 0, N_NODES, dtype=jnp.int32)
        dst = jax.random.randint(k3, (N_EDGES,), 0, N_NODES, dtype=jnp.int32)
        rel_type = jax.random.randint(k4, (N_EDGES,), 0, NUM_RELS, dtype=jnp.int32)
        norm = jax.random.uniform(k5, (N_EDGES, 1), dtype=jnp.float32)
        scale_w = np.sqrt(2.0) * np.sqrt(6.0 / (IN_DIM + OUT_DIM))
        bases = jax.random.uniform(k6, (NUM_BASES, IN_DIM, OUT_DIM), dtype=jnp.float32, minval=-scale_w, maxval=scale_w)
        scale_c = np.sqrt(2.0) * np.sqrt(6.0 / (NUM_RELS + NUM_BASES))
        w_comp = jax.random.uniform(k7, (NUM_RELS, NUM_BASES), dtype=jnp.float32, minval=-scale_c, maxval=scale_c)
        return {'h': h, 'src': src, 'dst': dst, 'rel_type': rel_type, 'norm': norm, 'bases': bases, 'w_comp': w_comp}
    _L0_gnn_all = _L0_gnn_setup()
    _L0_gnn_in = {k: v for k, v in _L0_gnn_all.items() if k in ('bases', 'w_comp')}
    del _L0_gnn_all

    def _L1_gnn_setup():
        import jax, jax.numpy as jnp
        import numpy as np
        N_NODES = 6250
        N_EDGES = 100000
        NUM_RELS = 16
        FEAT = 256
        OUT = 256
        key = jax.random.key(seed)
        ks = jax.random.split(key, 7)
        h = jax.random.normal(ks[0], (N_NODES, FEAT), dtype=jnp.float32)
        norm = jax.random.uniform(ks[1], (N_EDGES, 1), dtype=jnp.float32)
        weight = jax.random.normal(ks[2], (NUM_RELS, FEAT, OUT), dtype=jnp.float32) * 0.05
        gate_weight = jax.random.normal(ks[3], (NUM_RELS, FEAT, 1), dtype=jnp.float32) * 0.05
        src = jax.random.randint(ks[4], (N_EDGES,), 0, N_NODES)
        dst = jax.random.randint(ks[5], (N_EDGES,), 0, N_NODES)
        rel_type = jax.random.randint(ks[6], (N_EDGES,), 0, NUM_RELS)
        return {'h': h, 'norm': norm, 'weight': weight, 'gate_weight': gate_weight, 'src': src, 'dst': dst, 'rel_type': rel_type}
    _L1_gnn_all = _L1_gnn_setup()
    _L1_gnn_in = {k: v for k, v in _L1_gnn_all.items() if k in ('weight', 'gate_weight')}
    del _L1_gnn_all

    def _L2_gnn_setup():
        import jax, jax.numpy as jnp
        import numpy as np
        N = 6250
        E = 50000
        IN = 256
        H = 8
        D = 32
        EF = 3
        key = jax.random.key(seed)
        ks = jax.random.split(key, 8)
        x = jax.random.normal(ks[0], (N, IN), dtype=jnp.float32)
        edge_index = jax.random.randint(ks[1], (2, E), 0, N, dtype=jnp.int64)
        edge_attr = jax.random.normal(ks[2], (E, EF), dtype=jnp.float32)
        W = jax.random.normal(ks[3], (H * D, IN), dtype=jnp.float32) * np.float32(np.sqrt(2.0 / (IN + H * D)))
        a_src = jax.random.normal(ks[4], (H, D), dtype=jnp.float32) * np.float32(np.sqrt(2.0 / (H + D)))
        a_dst = jax.random.normal(ks[5], (H, D), dtype=jnp.float32) * np.float32(np.sqrt(2.0 / (H + D)))
        edge_W = jax.random.normal(ks[6], (H * D, EF), dtype=jnp.float32) * np.float32(np.sqrt(2.0 / (EF + H * D)))
        edge_b = jnp.zeros((H * D,), dtype=jnp.float32)
        bias = jnp.zeros((H * D,), dtype=jnp.float32)
        return {'x': x, 'W': W, 'a_src': a_src, 'a_dst': a_dst, 'edge_W': edge_W, 'edge_b': edge_b, 'bias': bias, 'edge_attr': edge_attr, 'edge_index': edge_index}
    _L2_gnn_all = _L2_gnn_setup()
    _L2_gnn_in = {k: v for k, v in _L2_gnn_all.items() if k in ('W', 'a_src', 'a_dst', 'edge_W', 'edge_b', 'bias')}
    del _L2_gnn_all

    def _L3_gnn_setup():
        import jax, jax.numpy as jnp
        import numpy as np
        N_NODES = 1250
        N_EDGES = 40000
        NUM_RELS = 20
        IN_FEAT = 256
        OUT_FEAT = 256
        key = jax.random.key(seed)
        k1, k2, k3, k4, k5, k6 = jax.random.split(key, 6)
        h = jax.random.normal(k1, (N_NODES, IN_FEAT), dtype=jnp.float32)
        gain = float(np.sqrt(2.0))
        limit = gain * float(np.sqrt(6.0 / (IN_FEAT + OUT_FEAT)))
        weight = jax.random.uniform(k2, (NUM_RELS, IN_FEAT, OUT_FEAT), dtype=jnp.float32, minval=-limit, maxval=limit)
        norm = jax.random.uniform(k3, (N_EDGES, 1), dtype=jnp.float32)
        edge_src = jax.random.randint(k4, (N_EDGES,), 0, N_NODES, dtype=jnp.int32)
        edge_dst = jax.random.randint(k5, (N_EDGES,), 0, N_NODES, dtype=jnp.int32)
        rel_type = jax.random.randint(k6, (N_EDGES,), 0, NUM_RELS, dtype=jnp.int32)
        return {'h': h, 'weight': weight, 'norm': norm, 'edge_src': edge_src, 'edge_dst': edge_dst, 'rel_type': rel_type}
    _L3_gnn_all = _L3_gnn_setup()
    _L3_gnn_in = {k: v for k, v in _L3_gnn_all.items() if k in ('weight',)}
    del _L3_gnn_all
    return {'x': x, 'src': src, 'dst': dst, 'edge_attr_3': edge_attr_3, 'edge_type_16': edge_type_16, 'edge_type_20': edge_type_20, 'edge_type_32': edge_type_32, 'edge_weight1': edge_weight1, 'L0_gnn_bases': _L0_gnn_in['bases'], 'L0_gnn_w_comp': _L0_gnn_in['w_comp'], 'L1_gnn_weight': _L1_gnn_in['weight'], 'L1_gnn_gate_weight': _L1_gnn_in['gate_weight'], 'L2_gnn_W': _L2_gnn_in['W'], 'L2_gnn_a_src': _L2_gnn_in['a_src'], 'L2_gnn_a_dst': _L2_gnn_in['a_dst'], 'L2_gnn_edge_W': _L2_gnn_in['edge_W'], 'L2_gnn_edge_b': _L2_gnn_in['edge_b'], 'L2_gnn_bias': _L2_gnn_in['bias'], 'L3_gnn_weight': _L3_gnn_in['weight']}

def reference(x, src, dst, edge_attr_3, edge_type_16, edge_type_20, edge_type_32, edge_weight1, L0_gnn_bases, L0_gnn_w_comp, L1_gnn_weight, L1_gnn_gate_weight, L2_gnn_W, L2_gnn_a_src, L2_gnn_a_dst, L2_gnn_edge_W, L2_gnn_edge_b, L2_gnn_bias, L3_gnn_weight):
    import jax
    import jax.numpy as jnp

    def _L0_gnn_ref(h, src, dst, rel_type, norm, bases, w_comp):
        import jax, jax.numpy as jnp
        import numpy as np
        N_NODES = 2500
        N_EDGES = 40000
        IN_DIM = 256
        OUT_DIM = 256
        NUM_RELS = 32
        NUM_BASES = 8
        weight = jnp.einsum('rb,bio->rio', w_comp, bases)
        xw = jnp.einsum('ni,rio->nro', h, weight)
        msg = xw[src, rel_type] * norm
        out = jax.ops.segment_sum(msg, dst, num_segments=h.shape[0])
        return jax.nn.relu(out)

    def _L1_gnn_ref(h, norm, weight, gate_weight, src, dst, rel_type):
        import jax, jax.numpy as jnp
        import numpy as np
        N_NODES = 6250
        N_EDGES = 100000
        NUM_RELS = 16
        FEAT = 256
        OUT = 256
        n_nodes = h.shape[0]
        all_msg = jnp.einsum('nf,rfo->rno', h, weight)
        msg = all_msg[rel_type, src] * norm
        all_gate = jnp.einsum('nf,rf->rn', h, gate_weight[..., 0])
        gate = jax.nn.sigmoid(all_gate[rel_type, src])[:, None]
        msg = msg * gate
        agg = jax.ops.segment_sum(msg, dst, num_segments=n_nodes)
        return jax.nn.relu(agg)

    def _L2_gnn_ref(x, W, a_src, a_dst, edge_W, edge_b, bias, edge_attr, edge_index):
        import jax, jax.numpy as jnp
        import numpy as np
        N = 6250
        E = 50000
        IN = 256
        H = 8
        D = 32
        EF = 3
        n = x.shape[0]
        h = (x @ W.T).reshape(n, H, D)
        src, dst = (edge_index[0], edge_index[1])
        h_src = h[src]
        h_dst = h[dst]
        alpha = jnp.einsum('ehd,hd->eh', h_src, a_src) + jnp.einsum('ehd,hd->eh', h_dst, a_dst)
        enc = jax.nn.relu(edge_attr @ edge_W.T + edge_b).reshape(-1, H, D)
        alpha = alpha + jnp.sum(enc * h_dst, axis=-1)
        alpha = jnp.where(alpha >= 0, alpha, 0.2 * alpha)
        amax = jax.ops.segment_max(alpha, dst, num_segments=n)
        ex = jnp.exp(alpha - amax[dst])
        denom = jax.ops.segment_sum(ex, dst, num_segments=n)
        attn = ex / jnp.maximum(denom[dst], 1e-10)
        out = jax.ops.segment_sum(h_src * attn[..., None], dst, num_segments=n)
        return out.reshape(n, H * D) + bias

    def _L3_gnn_ref(h, weight, norm, edge_src, edge_dst, rel_type):
        import jax, jax.numpy as jnp
        import numpy as np
        N_NODES = 1250
        N_EDGES = 40000
        NUM_RELS = 20
        IN_FEAT = 256
        OUT_FEAT = 256
        h_all = jnp.einsum('ni,rio->nro', h, weight)
        msg = h_all[edge_src, rel_type] * norm
        agg = jax.ops.segment_sum(msg, edge_dst, num_segments=h.shape[0])
        return jax.nn.relu(agg)
    edge_index = jnp.stack([src, dst])
    x = _layernorm(x + _L0_gnn_ref(x, src, dst, edge_type_32, edge_weight1, L0_gnn_bases, L0_gnn_w_comp), axis=-1)
    x = _layernorm(x + _L1_gnn_ref(x, edge_weight1, L1_gnn_weight, L1_gnn_gate_weight, src, dst, edge_type_16), axis=-1)
    x = _layernorm(x + _L2_gnn_ref(x, L2_gnn_W, L2_gnn_a_src, L2_gnn_a_dst, L2_gnn_edge_W, L2_gnn_edge_b, L2_gnn_bias, edge_attr_3, edge_index), axis=-1)
    x = _layernorm(x + _L3_gnn_ref(x, L3_gnn_weight, edge_weight1, src, dst, edge_type_20), axis=-1)
    return x

_drawn_inputs = setup_inputs


def setup_inputs(seed=0):
    import zlib

    import numpy as np

    out = dict(_drawn_inputs(seed))
    spreads = {'L2_gnn_edge_b': (0.0, 0.1), 'L2_gnn_bias': (0.0, 0.1)}
    factors = {}
    for name, (base, spread) in spreads.items():
        noise = np.random.default_rng([zlib.crc32(name.encode()), seed]).standard_normal(out[name].shape)
        drawn = base * np.exp(spread * noise) if base else spread * noise
        out[name] = jnp.asarray(drawn.astype(out[name].dtype))
    for name, factor in factors.items():
        out[name] = (out[name] * factor).astype(out[name].dtype)
    return out
```

```python
from contextlib import ExitStack

import concourse.bass as bass
from concourse import mybir

F32 = mybir.dt.float32
I32 = mybir.dt.int32
U8 = mybir.dt.uint8
ALU = mybir.AluOpType
ACT = mybir.ActivationFunctionType
AX = mybir.AxisListType

P = 128
D = 256
HEADS, HD = 8, 32
HROW = HEADS * (HD + 1)
GROW = HEADS + D
W2C = D + 2 * HEADS
BASES = 8
R0, R1, R3 = 32, 16, 20
BIG = 1.0e30
EPS = 1e-5
G = 8
U = 2 * G
FIELDS = 9
DST, SRC, T32, T16, T20, NORM, ATTR = range(7)


def build(nc, x, edges, dst_last, bases, w_compT, w1, gate1T, w2, w2T, a_src, a_dst, edge_wT,
          edge_b, bias2, w3, ident_one, out, stop=None):
    N = out.shape[0]
    NWIN = x.shape[0] // P
    NW1 = -(-N // P)
    TILES = edges.shape[0]
    STEPS = TILES + NW1 - 1
    KP = -(-STEPS // U) * U
    KC = -(-KP // P)
    ITERS = KP // U
    QS = P // HEADS
    QM = KP // QS
    NSC = KP * HEADS
    BLK = 4
    assert NWIN % 2 == 0 and KP % QS == 0 and QM % BLK == 0 and KP < 256 * 4

    table = nc.dram_tensor("table", (NWIN * P, R0 * D), F32).ap()
    w0_dram = nc.dram_tensor("w0_dram", (R0, D, D), F32).ap()
    attr_dram = nc.dram_tensor("attr_dram", (KC * P, 3, P), F32).ap()
    rows_dram = nc.dram_tensor("rows_dram", (KP // G, P, G * GROW), F32).ap()
    gat_table = nc.dram_tensor("gat_table", (NWIN * P, GROW), F32).ap()

    with ExitStack() as ctx:
        def sb(name, shape, dt=F32):
            return ctx.enter_context(nc.sbuf_tensor(name, shape, dt))

        def sem(name):
            return ctx.enter_context(nc.semaphore(name))

        X = sb("X", [P, NWIN, D])
        A = sb("A", [P, 2 * NSC + 16])
        W = sb("W", [P, 2 * NSC])
        dloc = sb("dloc", [P, KP])
        norm = sb("norm", [P, KP])
        srcf = sb("srcf", [P, KP])
        types = sb("types", [P, 3, KP], U8)
        idx = sb("idx", [P, KP], I32)
        win = sb("win", [1, KP], U8)
        ring = sb("ring", [P, U, GROW])
        onehot = sb("onehot", [P, G, P])
        turned = sb("turned", [P, 4, P])
        enc = A[:, NSC + 64:NSC + 64 + 2 * HROW].rearrange("p (e c) -> p e c", e=2)
        prod = A[:, NSC + 1024:NSC + 1024 + 2 * HROW].rearrange("p (e c) -> p e c", e=2)
        work = sb("work", [P, 2048])
        ident = sb("ident", [P, P])
        iota = sb("iota", [P, P])
        ix = sb("ix", [P, 2, G], I32)
        stat = sb("stat", [P, 4, NWIN])
        enc_w = sb("enc_w", [4, HROW])
        S = sb("S", [P, G, HEADS])
        small = sb("small", [P, 32])
        gate = sb("gate", [P, 2, R1])
        col = sb("col", [P, 8])
        ps = ctx.enter_context(nc.psum_tensor("ps", [P, 8, 512], F32))

        acc = A[:, 0:NWIN * GROW].rearrange("p (w c) -> p w c", c=GROW)
        stage = A[:, 0:4 * 5 * 512].rearrange("p (s c) -> p s c", s=4)
        xs = work[:, 0:512].rearrange("p (u c) -> p u c", u=2)
        xt = work[:, 512:1024].rearrange("p (u c n) -> p u c n", u=2, c=2)
        attrT = work[0:4, 0:2048].rearrange("p (h c) -> p h c", h=2)

        def w_rel(rels):
            return W[:, 0:2 * rels * D].rearrange("p (c n) -> p c n", c=2)

        alpha = A[:, 0:NSC].rearrange("p (k h) -> p k h", h=HEADS)
        hbuf = W[:, 0:NWIN * HROW].rearrange("p (w c) -> p w c", c=HROW)
        w2ext = work[:, 1024:1024 + 2 * W2C].rearrange("p (c o) -> p c o", c=2)
        gate_w = work[:, 1024:1024 + 2 * R1].rearrange("p (c r) -> p c r", c=2)
        gat_stage = A[:, 0:2 * W2C].rearrange("p (u c) -> p u c", u=2)
        w2nat = onehot[:, 0:4, :].rearrange("p (c a) b -> p c (a b)", c=2)
        gat_rows = gat_table.rearrange("(w p) c -> w p c", p=P)

        alphaT = W[:, 0:NSC]
        keyT = W[:, NSC:2 * NSC]
        maxT = W[:, NSC:2 * NSC]
        penalty = A[:, 0:NSC + 1]
        prefix = A[:, NSC + 8:2 * NSC + 8]
        ex = W[:, NSC:2 * NSC].rearrange("p (k h) -> p k h", h=HEADS)

        span = KC * P
        dl_i = A[0:NW1, 0:TILES].bitcast(I32)
        dl_f = A[0:NW1, 800:800 + TILES]
        k_i = A[0:NW1, 1600:1600 + span].bitcast(I32)
        k_f = A[0:NW1, 2500:2500 + span]
        below = A[0:NW1, 3400:3400 + span]
        junk = A[0:NW1, 4300:4300 + TILES]
        recf = A[:, 5200:5200 + KC * 5 * P].rearrange("p (k f e) -> p k f e", k=KC, f=5)
        wB = A[:, 12300:12300 + KP]
        rec = W[:, 0:KC * FIELDS * P].rearrange("p (k f e) -> p k f e", k=KC, f=FIELDS)
        w128_i = small[0:NW1, 0:1].bitcast(I32)
        w128_f = small[0:NW1, 1:2]
        below_count = small[0:NW1, 2:3]
        first_step = small[0:NW1, 3:4]
        ones_col = small[0:NW1, 16:17]
        ones_rows = onehot[0:NW1, 0, :]
        tile_f = stat[:, 0, 0:KC]
        step_f = stat[:, 1, 0:KC]
        step_i = stat[:, 2, 0:KC].bitcast(I32)
        tile_i = stat[:, 3, 0:KC].bitcast(I32)
        IB = D // 4
        HB = IB // 2
        Xflat = X[:, :, :].rearrange("p w c -> p (w c)")
        basesS = Xflat[0:4 * BASES, 0:HB * D]
        wout = Xflat[:, HB * D:HB * D + 4096].rearrange("p (s c) -> p s c", s=2)
        wsel = onehot[0:4 * BASES, 2, :]

        def rowv(n, m):
            return work[0:1, n * P:(n + m) * P]

        bar = sem("bar")
        dve_done = sem("dve_done")
        loaded = sem("loaded")
        stored = sem("stored")
        got = [sem(f"got{j}") for j in range(U)]
        claimed = sem("claimed")
        u_iota, u_ident, u_below, u_win, u_tile, u_rec, u_recf, u_turned, u_evac, u_attr, u_wsel, u_wrow, u_half, u_wps, u_wevac = (
            sem("u_" + n) for n in ("iota", "ident", "below", "win", "tile", "rec", "recf", "turned",
                                    "evac", "attr", "wsel", "wrow", "half", "wps", "wevac"))
        u_wst = [sem(f"u_wst{s}") for s in range(2)]
        ln_var, ln_std = sem("ln_var"), sem("ln_std")
        z_zero, z_ps, z_done = sem("z_zero"), sem("z_ps"), sem("z_done")

        class Pass:
            def __init__(self, name, weights, rels, r0, total, bpu, gated):
                self.weights, self.rels, self.r0, self.total, self.bpu, self.gated = weights, rels, r0, total, bpu, gated
                self.banks = rels * D // 512
                self.units = self.banks // bpu
                assert self.units == 2 and 2 * self.banks % 4 == 0
                (self.copied, self.turned, self.xt_ready, self.bank_full, self.bank_free, self.unit_full,
                 self.gate_full, self.gate_ready) = (sem(f"{name}_{n}") for n in (
                     "copied", "turned", "xt_ready", "bank_full", "bank_free", "unit_full", "gate_full", "gate_ready"))
                self.unit_free = [sem(f"{name}_unit_free{s}") for s in range(4)]
                self.table = table.rearrange("n c -> (n c)")[0:NWIN * P * total * D]

        class Walk:
            def __init__(self, name, nth, rels, tcol, table_):
                self.nth, self.rels, self.tcol, self.table = nth, rels, tcol, table_
                self.ix_free, self.ix_ready, self.onehot_ready, self.step_done, self.added = (
                    sem(f"{name}_{n}") for n in ("ix_free", "ix_ready", "onehot_ready", "step_done", "added"))

            def arrived(self, i):
                return i * 16 + (16 + 16 * ITERS * self.nth)

        p0a = Pass("p0a", w0_dram, R0 // 2, 0, R0, 4, False)
        p0b = Pass("p0b", w0_dram, R0 // 2, R0 // 2, R0, 4, False)
        p1 = Pass("p1", w1, R1, 0, R1, 4, True)
        p3 = Pass("p3", w3, R3, 0, R3, 5, False)
        walk0 = Walk("s0", 0, R0, 0, p0a.table)
        walk1 = Walk("s1", 1, R1, 1, p1.table)
        walk3 = Walk("s3", 3, R3, 2, p3.table)
        gw = Walk("sg", 2, 1, 0, None)
        g_copied, g_turned, g_xt, g_out, g_row, g_hbuf = (sem("g_" + n) for n in (
            "copied", "turned", "xt", "out", "row", "hbuf"))
        g_stored = [sem(f"g_stored{u}") for u in range(2)]
        (a_onehot, a_turned, a_copied, a_encps, a_relu, a_hd, a_prod, a_red, a_alpha) = (
            sem("a_" + n) for n in ("onehot", "turned", "copied", "encps", "relu", "hd", "prod", "red", "alpha"))
        a_attr = [sem(f"a_attr{h}") for h in range(2)]
        a_spill = [sem(f"a_spill{h}") for h in range(2)]
        m_copied, m_turned, m_evac, m_exp, m_back, m_out, m_cols, m_row = (sem("m_" + n) for n in (
            "copied", "turned", "evac", "exp", "back", "out", "cols", "row"))
        b_row = [sem(f"b_row{h}") for h in range(2)]
        b_exp, b_mult, b_onehot, b_done, b_added = (sem("b_" + n) for n in (
            "exp", "mult", "onehot", "done", "added"))

        PHASES = [("setup", None), ("load", p0a), ("pass", p0a), ("load", p0b), ("pass", p0b),
                  ("walk", walk0), ("norm", 0), ("load", p1), ("pass", p1), ("walk", walk1), ("norm", 1),
                  ("heads", None), ("gat_rows", None), ("scores", None), ("softmax", None), ("gather_sum", None),
                  ("norm", 2), ("load", p3), ("pass", p3), ("walk", walk3), ("norm", 3)]
        if stop is not None:
            PHASES = PHASES[:stop]

        def run(eng, parts):
            for n, (name, what) in enumerate(PHASES):
                if name in parts:
                    parts[name](what)
                eng.drain().then_inc(bar, 1)
                eng.wait_ge(bar, 5 * (n + 1))

        block = ctx.enter_context(nc.Block())

        @block.sync
        def _(sp):
            seen = [0]

            def load(dst, src):
                sp.dma_start(dst, src).then_inc(loaded, 16)
                seen[0] += 16

            def setup(_):
                load(dl_i, dst_last.partition_broadcast(NW1))
                sp.wait_ge(u_wsel, 1)
                for i4 in range(4):
                    sp.dma_start(wsel[i4 * BASES:(i4 + 1) * BASES, i4 * R0:(i4 + 1) * R0], w_compT).then_inc(u_wrow, 16)
                for half in range(2):
                    if half:
                        sp.wait_ge(u_wps, 16)
                    for i4 in range(4):
                        i0 = i4 * IB + half * HB
                        sp.dma_start(basesS[i4 * BASES:(i4 + 1) * BASES],
                                     bases[:, i0:i0 + HB, :].rearrange("b i o -> b (i o)")).then_inc(u_half, 16)
                    for n in range(4):
                        sp.wait_ge(u_wevac, 16 * half + 4 * n + 4)
                        for i4 in range(4):
                            i0 = i4 * IB + half * HB + n * 8
                            sp.dma_start(w0_dram[:, i0:i0 + 8, :].rearrange("r i o -> r (i o)"),
                                         wout[i4 * R0:(i4 + 1) * R0, n % 2, :]).then_inc(u_wst[n % 2], 16)
                for s in range(2):
                    sp.wait_ge(u_wst[s], 4 * 4 * 16)
                sp.wait_ge(u_rec, 16 * KC)
                for c in range(KC):
                    n = min(P, KP - c * P)
                    sp.dma_start(attr_dram[c * P:c * P + n], rec[0:n, c, ATTR:ATTR + 3, :]).then_inc(u_attr, 16)
                load(X[:, :, :], x.rearrange("(w p) c -> p w c", p=P))
                sp.wait_ge(u_attr, 16 * KC)
                sp.wait_ge(loaded, seen[0])

            def weights(ps_):
                for c in range(2):
                    load(w_rel(ps_.rels)[:, c, :].rearrange("p (r o) -> p r o", o=D),
                         ps_.weights[ps_.r0:ps_.r0 + ps_.rels, c * P:(c + 1) * P, :].rearrange("r p o -> p r o"))
                if ps_.gated:
                    load(gate_w[:, :, :], gate1T.rearrange("(c p) r -> p c r", p=P))
                sp.wait_ge(loaded, seen[0])

            def store_table(ps_):
                rows = ps_.table.rearrange("(w p c) -> w p c", p=P, c=ps_.total * D)
                with sp.Fori(0, NWIN // 2) as i:
                    for u in range(2):
                        for v in range(2):
                            s, c0 = 2 * u + v, ps_.r0 * D + v * ps_.bpu * 512
                            sp.wait_ge(ps_.unit_full, i * 4 + (s + 1))
                            sp.dma_start(rows[bass.ds(i * 2 + u, 1), :, c0:c0 + ps_.bpu * 512].squeeze(0),
                                         stage[:, s, 0:ps_.bpu * 512]).then_inc(ps_.unit_free[s], 16)
                for s in range(4):
                    sp.wait_ge(ps_.unit_free[s], 16 * (NWIN // 2) + 16)

            def norm_loads(layer):
                if layer == 1:
                    for c in range(2):
                        load(w2ext[:, c, HEADS:HEADS + D], w2T[c * P:(c + 1) * P, :])
                        load(w2nat[:, c, :], w2[c * P:(c + 1) * P, :])
                    sp.wait_ge(z_zero, 1)
                    with nc.allow_non_contiguous_dma(reason="a few hundred words"):
                        for h in range(HEADS):
                            c, q = h // 4, h % 4
                            load(small[q * HD:(q + 1) * HD, 16 * c + h:16 * c + h + 1], a_src[h:h + 1, :].rearrange("a d -> d a"))
                            load(small[q * HD:(q + 1) * HD, 16 * c + 8 + h:16 * c + 9 + h], a_dst[h:h + 1, :].rearrange("a d -> d a"))
                        load(enc_w[3:4, :].rearrange("p (h d) -> p h d", d=HD + 1)[:, :, HD:HD + 1], ident_one)
                    load(enc_w[0:3, :].rearrange("p (h d) -> p h d", d=HD + 1)[:, :, 0:HD], edge_wT.rearrange("k (h d) -> k h d", d=HD))
                    load(enc_w[3:4, :].rearrange("p (h d) -> p h d", d=HD + 1)[:, :, 0:HD], edge_b.rearrange("(a h d) -> a h d", a=1, d=HD))
                if layer == 2:
                    load(ring[:, 0, 0:D], bias2.partition_broadcast(P))
                sp.wait_ge(loaded, seen[0])
                if layer == 2:
                    sp.sem_inc(z_done, 1)

            def store_gat_rows(_):
                with sp.Fori(0, NWIN // 2) as i:
                    for u in range(2):
                        sp.wait_ge(g_row, i * 2 + (u + 3))
                        sp.dma_start(gat_rows[bass.ds(i * 2 + u, 1)].squeeze(0), gat_stage[:, u, 0:GROW]).then_inc(g_stored[u], 16)
                for u in range(2):
                    sp.wait_ge(g_stored[u], 16 * (NWIN // 2) + 16)

            def spill(_):
                with sp.Fori(0, ITERS) as i:
                    for h in range(2):
                        sp.wait_ge(a_encps, i * U + (h * G + G))
                        sp.dma_start(attrT[0:3, h, :].rearrange("c (k e) -> c k e", e=P),
                                     attr_dram[bass.ds(i * U + h * G, G)].rearrange("k c e -> c k e")).then_inc(a_attr[h], 16)
                    for h in range(2):
                        for j in range(G):
                            sp.wait_ge(got[h * G + j], gw.arrived(i))
                        sp.dma_start(rows_dram[bass.ds(i * 2 + h, 1)].squeeze(0),
                                     ring[:, h * G:(h + 1) * G, :].rearrange("p s c -> p (s c)")).then_inc(a_spill[h], 16)
                for h in range(2):
                    sp.wait_ge(a_spill[h], 16 * ITERS + 16)

            def reload(_):
                with sp.Fori(0, ITERS) as i:
                    for h in range(2):
                        sp.wait_ge(b_done, i * U + (h * G + G))
                        sp.dma_start(ring[:, h * G:(h + 1) * G, :].rearrange("p s c -> p (s c)"),
                                     rows_dram[bass.ds(i * 2 + h, 1)].squeeze(0)).then_inc(b_row[h], 16)

            run(sp, {"setup": setup, "load": weights, "pass": store_table, "norm": norm_loads,
                     "gat_rows": store_gat_rows, "scores": spill, "gather_sum": reload})
            full = N // P
            sp.dma_start(out[0:full * P, :].rearrange("(w p) c -> p w c", p=P), X[:, 0:full, :]).then_inc(stored, 16)
            sp.dma_start(out[full * P:N, :], X[0:N - full * P, full, :]).then_inc(stored, 16)
            sp.wait_ge(stored, 32)

        @block.gpsimd
        def _(pool):
            def setup(_):
                pool.iota(w128_i, [[0, 1]], base=0, channel_multiplier=P).then_inc(u_iota, 1)
                pool.iota(k_i, [[1, span]], base=0, channel_multiplier=0).then_inc(u_iota, 1)
                pool.iota(step_i, [[P, KC]], base=0, channel_multiplier=1).then_inc(u_iota, 1)
                pool.iota(iota[:, :], [[1, P]], base=0, channel_multiplier=0,
                          allow_small_or_imprecise_dtypes=True).then_inc(u_iota, 1)
                pool.memset(ident[:, :], 0.0).then_inc(u_ident, 1)
                pool.wait_ge(u_ident, 1)
                pool.affine_select(out=ident[:, :], in_=ident[:, :], compare_op=ALU.not_equal, fill=1.0,
                                   base=0, pattern=[[-1, P]], channel_multiplier=1).then_inc(u_ident, 1)
                pool.wait_ge(u_tile, 1)
                for c in range(KC):
                    pool.indirect_dma_start(out=rec[:, c, :, :].rearrange("p f e -> p (f e)").bitcast(I32), out_offset=None,
                                            in_=edges.rearrange("t f e -> t (f e)"),
                                            in_offset=bass.IndirectOffsetOnAxis(ap=tile_i[:, c:c + 1], axis=0)).then_inc(u_rec, 16)
                pool.wait_ge(u_rec, 16 * KC)

            def gather(src, width, wk):
                with pool.Fori(0, ITERS) as i:
                    for h in range(2):
                        pool.wait_ge(wk.ix_ready, i * 2 + (h + 1))
                        pool.sem_inc(claimed, 1)
                        for j in range(G):
                            pool.indirect_dma_start(out=ring[:, h * G + j, 0:width], out_offset=None, in_=src,
                                                    in_offset=bass.IndirectOffsetOnAxis(ap=ix[:, h, j:j + 1], axis=0)
                                                    ).then_inc(got[h * G + j], 16)

            def walk(wk):
                gather(wk.table.rearrange("(a o) -> a o", o=D), D, wk)

            def scores(_):
                gather(gat_table, GROW, gw)

            def weigh(_):
                with pool.Fori(0, ITERS) as i:
                    for h in range(2):
                        half = ring[:, h * G:(h + 1) * G, :]
                        rows = half[:, :, HEADS:GROW].rearrange("p k (h d) -> p k h d", d=HD)
                        pool.wait_ge(b_exp, i * 2 + (h + 1))
                        pool.tensor_tensor(rows, rows, half[:, :, 0:HEADS].unsqueeze(3).to_broadcast([P, G, HEADS, HD]),
                                           ALU.mult).then_inc(b_mult, 1)

            run(pool, {"setup": setup, "walk": walk, "scores": scores, "gather_sum": weigh})

        @block.vector
        def _(dve):
            done = [0]

            def ch(ins):
                ins.then_inc(dve_done, 1)
                done[0] += 1
                dve.wait_ge(dve_done, done[0])

            def setup(_):
                ch(dve.memset(wsel, 0.0))
                dve.sem_inc(u_wsel, 1)
                ch(dve.memset(ones_rows, 1.0))
                ch(dve.memset(ones_col, 1.0))
                dve.wait_ge(u_iota, 4)
                dve.wait_ge(loaded, 16)
                ch(dve.tensor_copy(dl_f, dl_i))
                ch(dve.tensor_copy(w128_f, w128_i))
                ch(dve.tensor_copy(k_f, k_i))
                ch(dve.tensor_scalar(junk, dl_f, w128_f, 0.0, ALU.is_lt, ALU.add, accum_out=below_count))
                ch(dve.scalar_tensor_tensor(first_step, w128_f, 1.0 / P, below_count, ALU.mult, ALU.add))
                ch(dve.tensor_scalar(below, k_f, first_step, None, ALU.is_ge))
                dve.sem_inc(u_below, 1)
                dve.wait_ge(u_win, 1)
                for c in range(2):
                    n = min(span // 2, KP - c * (span // 2))
                    ch(dve.tensor_scalar(wB[:, c * (span // 2):c * (span // 2) + n], ps[:, c, 0:n], -1.0, None, ALU.add))
                ch(dve.tensor_copy(win[0:1, :], wB[0:1, :]))
                ch(dve.tensor_copy(step_f, step_i))
                ch(dve.scalar_tensor_tensor(tile_f, ps[:, 2, 0:KC], -1.0, step_f, ALU.mult, ALU.add))
                ch(dve.tensor_scalar(tile_i, tile_f, 1.0, float(TILES - 1), ALU.add, ALU.min))
                dve.sem_inc(u_tile, 1)
                dve.wait_ge(u_rec, 16 * KC)
                ch(dve.tensor_copy(recf, rec[:, :, 0:5, :].bitcast(I32)))
                dve.sem_inc(u_recf, 1)
                dest = [dloc, srcf, types[:, 0, :], types[:, 1, :], types[:, 2, :], norm]
                for f in range(6):
                    for c in range(KC):
                        m, n = f * KC + c, min(P, KP - c * P)
                        dve.wait_ge(u_turned, m + 1)
                        dve.tensor_copy(dest[f][:, c * P:c * P + n], ps[:, 3 + m % 3, 0:n]).then_inc(u_evac, 1)
                dve.wait_ge(u_evac, 6 * KC)
                ch(dve.scalar_tensor_tensor(dloc[:, :], wB, -float(P), dloc[:, :], ALU.mult, ALU.add))
                ch(dve.memset(dloc[:, STEPS:KP], -1.0))

            def windows_to_xt(copied, turned, xt_ready):
                with dve.Fori(0, NWIN // 2) as i:
                    for u in range(2):
                        dve.tensor_copy(xs[:, u, :], X[:, bass.ds(i * 2 + u, 1), :].squeeze(1)).then_inc(copied, 1)
                    for u in range(2):
                        dve.wait_ge(turned, i * 2 + (u + 1))
                        dve.tensor_copy(xt[:, u, :, :], ps[:, 6 + u, 0:D].rearrange("p (c n) -> p c n", c=2)).then_inc(xt_ready, 1)

            def copies(ps_):
                windows_to_xt(ps_.copied, ps_.turned, ps_.xt_ready)

            def window_registers(i, h):
                _, regs = nc.values_load_multi_w_load_instructions(
                    win[0:1, bass.ds(i * U + h * G, G)], engines=[dve.engine], min_val=0, max_val=NWIN - 1,
                    skip_runtime_bounds_check_because="a step's window counts windows that have begun, at most all of them")
                return regs

            def add_steps(i, h, width, step_done, added):
                regs = window_registers(i, h)
                for j in range(G):
                    dve.wait_ge(step_done, i * U + (h * G + j + 1 + U))
                    dve.wait_ge(added, i * U + (h * G + j + G))
                    a = acc[:, bass.ds(regs[j], 1), 0:width].squeeze(1)
                    dve.tensor_tensor(a, a, ps[:, j, 0:width], ALU.add).then_inc(added, 1)

            def walk(wk):
                ch(dve.scalar_tensor_tensor(idx[:, :], srcf[:, :], float(wk.rels), types[:, wk.tcol, :], ALU.mult, ALU.add))
                ch(dve.memset(A[:, 0:NWIN * GROW], 0.0))
                dve.sem_inc(wk.ix_free, 1)
                dve.sem_inc(wk.added, G)
                with dve.Fori(0, ITERS) as i:
                    for h in range(2):
                        for j in range(G):
                            s = i * U + (h * G + j)
                            dve.wait_ge(wk.step_done, i * U + (h * G + j + G + 1))
                            dve.tensor_scalar(onehot[:, j, :], iota[:, :], dloc[:, bass.ds(s, 1)], norm[:, bass.ds(s, 1)],
                                              ALU.is_equal, ALU.mult).then_inc(wk.onehot_ready, 1)
                        add_steps(i, h, D, wk.step_done, wk.added)
                dve.wait_ge(wk.added, KP + G)

            def residual_norm(layer):
                mean, var, rstd = stat[:, 0, :], stat[:, 1, :], stat[:, 2, :]
                if layer == 1:
                    ch(dve.memset(small[:, :], 0.0))
                    ch(dve.memset(enc_w[:, :], 0.0))
                    dve.sem_inc(z_zero, 1)
                if layer == 2:
                    a = acc[:, :, HEADS:GROW]
                    ch(dve.tensor_scalar(acc[:, :, 0:HEADS], acc[:, :, 0:HEADS], 1e-10, None, ALU.max))
                    ch(dve.reciprocal(acc[:, :, 0:HEADS], acc[:, :, 0:HEADS]))
                    ah = a.rearrange("p w (h d) -> p w h d", d=HD)
                    ch(dve.tensor_tensor(ah, ah, acc[:, :, 0:HEADS].unsqueeze(3).to_broadcast([P, NWIN, HEADS, HD]), ALU.mult))
                    dve.wait_ge(z_done, 1)
                    ch(dve.tensor_tensor(a, a, ring[:, 0:1, 0:D].to_broadcast([P, NWIN, D]), ALU.add))
                    ch(dve.tensor_tensor(X[:, :, :], a, X[:, :, :], ALU.add))
                else:
                    ch(dve.scalar_tensor_tensor(X[:, :, :], acc[:, :, 0:D], 0.0, X[:, :, :], ALU.max, ALU.add))
                ch(dve.tensor_reduce(mean, X[:, :, :], AX.X, ALU.add))
                ch(dve.tensor_scalar(mean, mean, 1.0 / D, None, ALU.mult))
                ch(dve.tensor_tensor(X[:, :, :], X[:, :, :], mean.unsqueeze(2).to_broadcast([P, NWIN, D]), ALU.subtract))
                ch(dve.tensor_tensor(acc[:, :, 0:D], X[:, :, :], X[:, :, :], ALU.mult))
                ch(dve.tensor_reduce(var, acc[:, :, 0:D], AX.X, ALU.add))
                ch(dve.tensor_scalar(var, var, 1.0 / D, EPS, ALU.mult, ALU.add))
                dve.sem_inc(ln_var, 1)
                dve.wait_ge(ln_std, layer + 1)
                ch(dve.reciprocal(rstd, rstd))
                ch(dve.tensor_tensor(X[:, :, :], X[:, :, :], rstd.unsqueeze(2).to_broadcast([P, NWIN, D]), ALU.mult))

            def heads(_):
                for c in range(2):
                    dve.wait_ge(z_ps, c + 1)
                    ch(dve.tensor_copy(w2ext[:, c, 0:HEADS], ps[:, c, 0:HEADS]))
                    ch(dve.tensor_copy(w2ext[:, c, HEADS + D:W2C], ps[:, c, HEADS:2 * HEADS]))

            def gat_rows_(_):
                dve.sem_inc(g_hbuf, 2)
                with dve.Fori(0, NWIN // 2) as i:
                    for u in range(2):
                        dve.tensor_copy(xs[:, u, :], X[:, bass.ds(i * 2 + u, 1), :].squeeze(1)).then_inc(g_copied, 1)
                    for u in range(2):
                        dve.wait_ge(g_turned, i * 2 + (u + 1))
                        dve.tensor_copy(xt[:, u, :, :], ps[:, 6 + u, 0:D].rearrange("p (c n) -> p c n", c=2)).then_inc(g_xt, 1)
                    for u in range(2):
                        dve.wait_ge(g_row, i * 2 + (u + 3))
                        row = hbuf[:, bass.ds(i * 2 + u, 1), :].squeeze(1).rearrange("p (h d) -> p h d", d=HD + 1)
                        dve.tensor_copy(row[:, :, 0:HD], gat_stage[:, u, HEADS:HEADS + D].rearrange("p (h d) -> p h d", d=HD))
                        dve.tensor_copy(row[:, :, HD:HD + 1], gat_stage[:, u, HEADS + D:W2C].unsqueeze(2)).then_inc(g_hbuf, 1)

            def scores(_):
                ch(dve.tensor_copy(idx[:, :], srcf[:, :]))
                dve.sem_inc(gw.ix_free, 1)
                ch(dve.memset(work[0:4, :], 1.0))
                dve.sem_inc(a_encps, U)
                dve.sem_inc(a_prod, 2)
                dve.sem_inc(a_red, 2)
                dve.sem_inc(a_alpha, 2)
                with dve.Fori(0, ITERS) as i:
                    for h in range(2):
                        for j in range(G):
                            s = i * U + (h * G + j)
                            dve.wait_ge(a_turned, s + 1)
                            dve.tensor_scalar(onehot[:, j, :], iota[:, :], dloc[:, bass.ds(s, 1)], None,
                                              ALU.is_equal).then_inc(a_onehot, 1)
                        for j in range(G):
                            e, s = j % 2, i * U + h * G + j
                            dve.wait_ge(a_hd, s + 5)
                            dve.wait_ge(a_relu, s + 3)
                            dve.wait_ge(a_red, s + 1)
                            dve.tensor_tensor(prod[:, e, :], enc[:, e, :], ps[:, 2 + e, 0:HROW], ALU.mult).then_inc(a_prod, 1)
                            dve.wait_ge(a_prod, s + 3)
                            dve.wait_ge(a_alpha, i * 2 + (h + 2))
                            dve.tensor_reduce(S[:, j, :], prod[:, e, :].rearrange("p (h d) -> p h d", d=HD + 1), AX.X,
                                              ALU.add).then_inc(a_red, 1)
                        dve.wait_ge(a_red, i * U + (h * G + G + 2))
                        for j in range(G):
                            dve.wait_ge(got[h * G + j], gw.arrived(i))
                        dve.tensor_tensor(alpha[:, bass.ds(i * U + h * G, G), :], S[:, :, :],
                                          ring[:, h * G:(h + 1) * G, 0:HEADS], ALU.add).then_inc(a_alpha, 1)
                dve.wait_ge(a_alpha, 2 * ITERS + 2)

            def softmax(_):
                ch(dve.scalar_tensor_tensor(A[:, 0:NSC], A[:, 0:NSC], 0.2, A[:, 0:NSC], ALU.mult, ALU.max))
                dve.sem_inc(m_turned, 1)
                av = A[:, 0:NSC].rearrange("p (q m h) -> p q m h", q=QS, h=HEADS)
                dv = dloc[:, :].rearrange("p (q m) -> p q m", q=QS)
                with dve.Fori(0, QM // BLK) as i:
                    dve.wait_ge(m_turned, i + 1)
                    for b in range(BLK):
                        dst = work[:, b * P:(b + 1) * P].rearrange("p (q h) -> p q h", h=HEADS)
                        key = work[:, 512 + b * P:512 + (b + 1) * P].rearrange("p (q h) -> p q h", h=HEADS)
                        dve.tensor_copy(dst, av[:, :, bass.ds(i * BLK + b, 1), :].squeeze(2))
                        ins = dve.tensor_copy(key, dv[:, :, bass.ds(i * BLK + b, 1)].to_broadcast([P, QS, HEADS]))
                    ins.then_inc(m_copied, 1)
                dve.wait_ge(m_evac, 2 * (QM // BLK) + 2)
                ch(dve.tensor_tensor(penalty[:, 1:NSC], keyT[:, 1:NSC], keyT[:, 0:NSC - 1], ALU.not_equal))
                ch(dve.tensor_scalar(penalty[:, 1:NSC], penalty[:, 1:NSC], -BIG, None, ALU.mult))
                ch(dve.tensor_reduce(col[:, 0:1], penalty[:, 1:NSC], AX.X, ALU.min))
                ch(dve.tensor_copy(col[:, 1:2], keyT[:, 0:1]))
                ch(dve.tensor_copy(col[:, 2:3], keyT[:, NSC - 1:NSC]))
                ch(dve.memset(penalty[:, 0:1], -BIG))
                ch(dve.tensor_tensor_scan(prefix, penalty[:, 0:NSC], alphaT, -BIG, ALU.add, ALU.max))
                ch(dve.tensor_copy(col[:, 3:4], prefix[:, NSC - 1:NSC]))
                dve.sem_inc(m_cols, 1)
                dve.wait_ge(m_row, 1)
                ch(dve.tensor_copy(rowv(0, 4), ps[0:1, 0, 0:4 * P]))
                whole, fk, lk, tail, link, nlink, pen_q, car = (rowv(n, 1) for n in range(8))
                H8 = HEADS
                ch(dve.memset(link, 0.0))
                ch(dve.tensor_tensor(link[:, H8:P], fk[:, H8:P], lk[:, 0:P - H8], ALU.is_equal))
                ch(dve.tensor_scalar(link, link, -1.0, BIG, ALU.add, ALU.mult))
                ch(dve.memset(nlink, -BIG))
                ch(dve.tensor_copy(nlink[:, 0:P - H8], link[:, H8:P]))
                by_head = "o (q h) -> o h q"
                a_hq, b_hq, c_hq = (rowv(n, 1) for n in (8, 9, 10))
                hq = "o (h q) -> o h q"

                def carries(lnk, ends, rev, out_row):
                    ch(dve.tensor_tensor(pen_q, lnk, whole, ALU.add))
                    for src_, dst_ in ((pen_q, a_hq), (ends, b_hq)):
                        v = src_.rearrange(by_head, h=HEADS)
                        v = v[:, :, ::-1] if rev else v
                        ch(dve.tensor_copy(dst_.rearrange(hq, h=HEADS), v))
                    ch(dve.tensor_tensor_scan(c_hq, a_hq, b_hq, -BIG, ALU.add, ALU.max))
                    ch(dve.memset(out_row, -BIG))
                    o = out_row.rearrange(by_head, h=HEADS)
                    cv = c_hq.rearrange(hq, h=HEADS)
                    if rev:
                        ch(dve.tensor_copy(o[:, :, 0:QS - 1], cv[:, :, 0:QS - 1][:, :, ::-1]))
                    else:
                        ch(dve.tensor_copy(o[:, :, 1:QS], cv[:, :, 0:QS - 1]))

                carries(link, tail, False, car)
                dve.sem_inc(m_cols, 1)
                dve.wait_ge(m_row, 2)
                ch(dve.tensor_copy(col[:, 4:7], ps[:, 1, 0:3]))
                ch(dve.tensor_copy(penalty[:, 0:1], col[:, 4:5]))
                ch(dve.tensor_copy(penalty[:, NSC:NSC + 1], col[:, 5:6]))
                ch(dve.tensor_tensor_scan(prefix, penalty[:, 0:NSC], alphaT, col[:, 6:7], ALU.add, ALU.max))
                ch(dve.tensor_tensor_scan(maxT[:, ::-1], penalty[:, 1:NSC + 1][:, ::-1], prefix[:, ::-1], -BIG, ALU.add, ALU.max))
                ch(dve.tensor_copy(col[:, 3:4], maxT[:, 0:1]))
                dve.sem_inc(m_cols, 1)
                dve.wait_ge(m_row, 3)
                ch(dve.tensor_copy(tail, ps[0:1, 0, 0:P]))
                carries(nlink, tail, True, car)
                dve.sem_inc(m_cols, 1)
                dve.wait_ge(m_row, 4)
                ch(dve.tensor_copy(col[:, 6:7], ps[:, 1, 0:1]))
                ch(dve.tensor_tensor_scan(maxT[:, ::-1], penalty[:, 1:NSC + 1][:, ::-1], prefix[:, ::-1], col[:, 6:7], ALU.add, ALU.max))
                ch(dve.tensor_tensor(alphaT, alphaT, maxT, ALU.subtract))
                dve.sem_inc(m_back, 1)
                dve.sem_inc(m_out, 1)
                exq = W[:, NSC:2 * NSC].rearrange("p (q m h) -> p q m h", q=QS, h=HEADS)
                with dve.Fori(0, QM // BLK) as i:
                    dve.wait_ge(m_back, i + 2)
                    for b in range(BLK):
                        ins = dve.tensor_copy(exq[:, :, bass.ds(i * BLK + b, 1), :].squeeze(2),
                                              ps[:, 2, b * P:(b + 1) * P].rearrange("p (q h) -> p q h", h=HEADS))
                    ins.then_inc(m_out, 1)
                ch(dve.memset(A[:, 0:NWIN * GROW], 0.0))

            def gather_sum(_):
                dve.sem_inc(b_added, G)
                with dve.Fori(0, ITERS) as i:
                    for h in range(2):
                        for j in range(G):
                            s = i * U + (h * G + j)
                            dve.wait_ge(b_done, i * U + (h * G + j + G + 1))
                            dve.tensor_scalar(onehot[:, j, :], iota[:, :], dloc[:, bass.ds(s, 1)], None,
                                              ALU.is_equal).then_inc(b_onehot, 1)
                        add_steps(i, h, GROW, b_done, b_added)
                dve.wait_ge(b_added, KP + G)

            run(dve, {"setup": setup, "pass": copies, "walk": walk, "norm": residual_norm, "heads": heads,
                      "gat_rows": gat_rows_, "scores": scores, "softmax": softmax, "gather_sum": gather_sum})

        @block.scalar
        def _(act):
            def setup(_):
                for m in range(32):
                    n = m // 4
                    act.wait_ge(u_wps, m + 1)
                    if m % 4 == 0 and n >= 2:
                        act.wait_ge(u_wst[n % 2], 64 * (n // 2))
                    act.activation(wout[:, n % 2, (m % 4) * 512:(m % 4 + 1) * 512], ps[:, 6 + m % 2, :], ACT.Copy).then_inc(u_wevac, 1)

            def evacuate(ps_):
                act.sem_inc(ps_.bank_free, 4)
                if ps_.gated:
                    act.sem_inc(ps_.gate_ready, 2)
                for s in range(4):
                    act.sem_inc(ps_.unit_free[s], 16)
                with act.Fori(0, NWIN // 2) as i:
                    for u in range(2):
                        if ps_.gated:
                            act.wait_ge(ps_.gate_full, i * 2 + (u + 1))
                            act.activation(gate[:, u, :], ps[:, 4 + u, 0:R1], ACT.Sigmoid).then_inc(ps_.gate_ready, 1)
                            act.wait_ge(ps_.gate_ready, i * 2 + (u + 3))
                        for v in range(2):
                            s = 2 * u + v
                            act.wait_ge(ps_.unit_free[s], i * 16 + 16)
                            for b in range(ps_.bpu):
                                m = s * ps_.bpu + b
                                dst = stage[:, s, b * 512:(b + 1) * 512]
                                act.wait_ge(ps_.bank_full, i * (4 * ps_.bpu) + (m + 1))
                                if ps_.gated:
                                    r = (v * ps_.bpu + b) * 2
                                    act.activation(dst[:, 0:D], ps[:, m % 4, 0:D], ACT.Copy, scale=gate[:, u, r:r + 1])
                                    ins = act.activation(dst[:, D:512], ps[:, m % 4, D:512], ACT.Copy, scale=gate[:, u, r + 1:r + 2])
                                else:
                                    ins = act.activation(dst, ps[:, m % 4, :], ACT.Copy)
                                ins.then_inc(ps_.bank_free, 1)
                            act.wait_ge(ps_.bank_free, i * (4 * ps_.bpu) + ((s + 1) * ps_.bpu + 4))
                            act.sem_inc(ps_.unit_full, 1)

            def indices(wk):
                act.wait_ge(wk.ix_free, 1)
                with act.Fori(0, ITERS) as i:
                    for h in range(2):
                        act.wait_ge(wk.step_done, i * U + (h * G + G))
                        act.activation(ix[:, h, :], idx[:, bass.ds(i * U + h * G, G)], ACT.Copy).then_inc(wk.ix_ready, 1)

            def std(layer):
                act.wait_ge(ln_var, layer + 1)
                act.activation(stat[:, 2, :], stat[:, 1, :], ACT.Sqrt).then_inc(ln_std, 1)

            def gat_rows_(_):
                act.sem_inc(g_row, 2)
                for u in range(2):
                    act.sem_inc(g_stored[u], 16)
                with act.Fori(0, NWIN // 2) as i:
                    for u in range(2):
                        act.wait_ge(g_out, i * 2 + (u + 1))
                        act.wait_ge(g_stored[u], i * 16 + 16)
                        act.wait_ge(g_hbuf, i * 2 + (u + 1))
                        act.activation(gat_stage[:, u, :], ps[:, u, 0:W2C], ACT.Copy).then_inc(g_row, 1)

            def scores(_):
                act.wait_ge(gw.ix_free, 1)
                act.sem_inc(a_copied, 2)
                act.sem_inc(a_relu, 2)
                for h in range(2):
                    act.sem_inc(a_spill[h], 16)
                with act.Fori(0, ITERS) as i:
                    for h in range(2):
                        act.wait_ge(a_alpha, i * 2 + (h + 1))
                        act.wait_ge(a_spill[h], i * 16 + 16)
                        act.activation(ix[:, h, :], idx[:, bass.ds(i * U + h * G, G)], ACT.Copy).then_inc(gw.ix_ready, 1)
                        for j in range(G):
                            s, e, f = i * U + h * G + j, j % 2, j % 4
                            act.wait_ge(a_turned, s + (1 + G))
                            act.wait_ge(a_hd, s + 1)
                            act.activation(turned[:, f, :], ps[:, e, 0:P], ACT.Copy).then_inc(a_copied, 1)
                            act.wait_ge(a_encps, s + (1 + U))
                            act.wait_ge(a_prod, s + 1)
                            act.activation(enc[:, e, :], ps[:, 4 + e, 0:HROW], ACT.Relu).then_inc(a_relu, 1)

            def softmax(_):
                act.sem_inc(m_evac, 2)
                with act.Fori(0, QM // BLK) as i:
                    act.wait_ge(m_turned, i + 2)
                    act.activation(W[:, bass.ds(i * 512, 512)], ps[:, 0, :], ACT.Copy).then_inc(m_evac, 1)
                    act.activation(W[:, bass.ds(i * 512 + NSC, 512)], ps[:, 1, :], ACT.Copy).then_inc(m_evac, 1)
                with act.Fori(0, QM // BLK) as i:
                    act.wait_ge(m_back, i + 1)
                    act.activation(work[:, 0:512], W[:, bass.ds(i * 512, 512)], ACT.Exp).then_inc(m_exp, 1)

            def exps(_):
                with act.Fori(0, ITERS) as i:
                    for h in range(2):
                        act.wait_ge(b_row[h], i * 16 + 16)
                        act.activation(ring[:, h * G:(h + 1) * G, 0:HEADS], ex[:, bass.ds(i * U + h * G, G), :], ACT.Copy).then_inc(b_exp, 1)

            run(act, {"setup": setup, "pass": evacuate, "walk": indices, "norm": std, "gat_rows": gat_rows_,
                      "scores": scores, "softmax": softmax, "gather_sum": exps})

        @block.tensor
        def _(pe):
            def setup(_):
                pe.wait_ge(u_below, 1)
                for c in range(2):
                    pe.matmul(ps[:, c, 0:span // 2], ones_rows, below[:, c * (span // 2):(c + 1) * (span // 2)], start=True, stop=True)
                for c in range(KC):
                    ins = pe.matmul(ps[:, 2, c:c + 1], below[:, c * P:(c + 1) * P], ones_col, start=True, stop=True)
                ins.then_inc(u_win, 1)
                pe.wait_ge(u_wrow, 64)
                for m in range(32):
                    if m % 16 == 0:
                        pe.wait_ge(u_half, 64 * (m // 16 + 1))
                    if m >= 2:
                        pe.wait_ge(u_wevac, m - 1)
                    pe.matmul(ps[:, 6 + m % 2, :], wsel, basesS[:, (m % 16) * 512:(m % 16 + 1) * 512], start=True, stop=True).then_inc(u_wps, 1)
                pe.wait_ge(u_recf, 1)
                pe.wait_ge(u_ident, 2)
                for f in range(6):
                    for c in range(KC):
                        m = f * KC + c
                        if m >= 3:
                            pe.wait_ge(u_evac, m - 2)
                        pe.transpose(ps[:, 3 + m % 3, 0:P], recf[:, c, f, :] if f < 5 else rec[:, c, NORM, :], ident[:, :]).then_inc(u_turned, 1)

            def turn(i, copied, turned_):
                for u in range(2):
                    pe.wait_ge(copied, i * 2 + (u + 1))
                    for c in range(2):
                        ins = pe.transpose(ps[:, 6 + u, c * P:(c + 1) * P], xs[:, u, c * P:(c + 1) * P], ident[:, :])
                    ins.then_inc(turned_, 1)

            def products(ps_):
                w = w_rel(ps_.rels)
                with pe.Fori(0, NWIN // 2) as i:
                    turn(i, ps_.copied, ps_.turned)
                    for u in range(2):
                        pe.wait_ge(ps_.xt_ready, i * 2 + (u + 1))
                        if ps_.gated:
                            pe.wait_ge(ps_.gate_ready, i * 2 + (u + 1))
                            for c in range(2):
                                ins = pe.matmul(ps[:, 4 + u, 0:R1], xt[:, u, c, :], gate_w[:, c, :],
                                                start=(c == 0), stop=(c == 1))
                            ins.then_inc(ps_.gate_full, 1)
                        for b in range(ps_.banks):
                            m = u * ps_.banks + b
                            pe.wait_ge(ps_.bank_free, i * (2 * ps_.banks) + (m + 1))
                            for c in range(2):
                                ins = pe.matmul(ps[:, m % 4, :], xt[:, u, c, :], w[:, c, b * 512:(b + 1) * 512],
                                                start=(c == 0), stop=(c == 1))
                            ins.then_inc(ps_.bank_full, 1)

            def walk(wk):
                pe.sem_inc(wk.step_done, U)
                with pe.Fori(0, ITERS) as i:
                    for h in range(2):
                        for j in range(G):
                            s = i * U + (h * G + j)
                            pe.wait_ge(got[h * G + j], wk.arrived(i))
                            pe.wait_ge(wk.onehot_ready, s + 1)
                            pe.wait_ge(wk.added, s + 1)
                            pe.matmul(ps[:, j, 0:D], onehot[:, j, :], ring[:, h * G + j, 0:D], start=True, stop=True).then_inc(wk.step_done, 1)

            def heads(_):
                for c in range(2):
                    for k in range(2):
                        ins = pe.matmul(ps[:, c, 0:2 * HEADS], w2nat[:, k, c * P:(c + 1) * P], small[:, 16 * k:16 * k + 16],
                                        start=(k == 0), stop=(k == 1))
                    ins.then_inc(z_ps, 1)

            def gat_rows_(_):
                with pe.Fori(0, NWIN // 2) as i:
                    turn(i, g_copied, g_turned)
                    for u in range(2):
                        pe.wait_ge(g_xt, i * 2 + (u + 1))
                        pe.wait_ge(g_row, i * 2 + (u + 1))
                        for c in range(2):
                            ins = pe.matmul(ps[:, u, 0:W2C], xt[:, u, c, :], w2ext[:, c, :], start=(c == 0), stop=(c == 1))
                        ins.then_inc(g_out, 1)

            def scores(_):
                pe.sem_inc(a_turned, G)
                pe.sem_inc(a_hd, 4)

                def turn_onehot(s, j):
                    pe.wait_ge(a_onehot, s + 1)
                    pe.wait_ge(a_copied, s + 1)
                    pe.transpose(ps[:, j % 2, 0:P], onehot[:, j, :], ident[:, :]).then_inc(a_turned, 1)

                with pe.Fori(0, ITERS) as i:
                    for h in range(2):
                        _, regs = nc.values_load_multi_w_load_instructions(
                            win[0:1, bass.ds(i * U + h * G, G)], engines=[pe.engine], min_val=0, max_val=NWIN - 1,
                            skip_runtime_bounds_check_because="a step's window counts windows that have begun, at most all of them")
                        turn_onehot(i * U + h * G, 0)
                        for j in range(G):
                            s, e = i * U + h * G + j, j % 2
                            if j + 1 < G:
                                turn_onehot(s + 1, j + 1)
                            if j == 0:
                                pe.wait_ge(a_attr[h], i * 16 + 16)
                            pe.wait_ge(a_relu, s + 1)
                            pe.matmul(ps[:, 4 + e, 0:HROW], attrT[:, h, j * P:(j + 1) * P], enc_w[:, :], start=True, stop=True).then_inc(a_encps, 1)
                            pe.wait_ge(a_copied, s + 3)
                            pe.wait_ge(a_prod, s + 1)
                            pe.matmul(ps[:, 2 + e, 0:HROW], turned[:, j % 4, :], hbuf[:, bass.ds(regs[j], 1), :].squeeze(1),
                                      start=True, stop=True).then_inc(a_hd, 1)

            def softmax(_):
                with pe.Fori(0, QM // BLK) as i:
                    pe.wait_ge(m_copied, i + 1)
                    pe.wait_ge(m_evac, i * 2 + 2)
                    for b in range(BLK):
                        pe.transpose(ps[:, 0, b * P:(b + 1) * P], work[:, b * P:(b + 1) * P], ident[:, :])
                        ins = pe.transpose(ps[:, 1, b * P:(b + 1) * P], work[:, 512 + b * P:512 + (b + 1) * P], ident[:, :])
                    ins.then_inc(m_turned, 1)
                one = ident[0:1, 0:1]
                for r in range(2):
                    pe.wait_ge(m_cols, 2 * r + 1)
                    for n in ((0, 1, 2, 3) if r == 0 else (3,)):
                        k = n if r == 0 else 0
                        ins = pe.transpose(ps[0:1, 0, k * P:(k + 1) * P], col[:, n:n + 1], ident[:, :])
                    ins.then_inc(m_row, 1)
                    pe.wait_ge(m_cols, 2 * r + 2)
                    for k, n in (((0, 4), (1, 5), (2, 7)) if r == 0 else ((0, 7),)):
                        ins = pe.transpose(ps[:, 1, k:k + 1], rowv(n, 1), one)
                    ins.then_inc(m_row, 1)
                with pe.Fori(0, QM // BLK) as i:
                    pe.wait_ge(m_exp, i + 1)
                    pe.wait_ge(m_out, i + 1)
                    for b in range(BLK):
                        ins = pe.transpose(ps[:, 2, b * P:(b + 1) * P], work[:, b * P:(b + 1) * P], ident[:, :])
                    ins.then_inc(m_back, 1)

            def gather_sum(_):
                pe.sem_inc(b_done, U)
                with pe.Fori(0, ITERS) as i:
                    for h in range(2):
                        for j in range(G):
                            s = i * U + (h * G + j)
                            if j == 0:
                                pe.wait_ge(b_mult, i * 2 + (h + 1))
                            pe.wait_ge(b_onehot, s + 1)
                            pe.wait_ge(b_added, s + 1)
                            pe.matmul(ps[:, j, 0:GROW], onehot[:, j, :], ring[:, h * G + j, :], start=True, stop=True).then_inc(b_done, 1)

            run(pe, {"setup": setup, "pass": products, "walk": walk, "heads": heads, "gat_rows": gat_rows_,
                     "scores": scores, "softmax": softmax, "gather_sum": gather_sum})


def kernel(**inputs):
    import numpy as np
    import concourse.bacc as bacc
    from concourse.bass_utils import run_bass_kernel_spmd

    v = {k: np.asarray(a) for k, a in inputs.items()}
    E, N = v["dst"].shape[0], v["x"].shape[0]
    tiles = -(-E // P)
    pad = tiles * P - E

    def edge_rows(a, fill=0):
        return np.pad(np.ascontiguousarray(a), (0, pad), constant_values=fill).view(np.int32).reshape(tiles, 1, P)

    attr = v["edge_attr_3"]
    edges = np.concatenate(
        [edge_rows(v["dst"], 1 << 14), edge_rows(v["src"]), edge_rows(v["edge_type_32"]), edge_rows(v["edge_type_16"]),
         edge_rows(v["edge_type_20"]), edge_rows(v["edge_weight1"][:, 0])] + [edge_rows(attr[:, c]) for c in range(3)], axis=1)
    windows = -(-N // (2 * P)) * 2
    arrays = {
        "x": np.pad(v["x"], ((0, windows * P - N), (0, 0))), "edges": edges,
        "dst_last": np.ascontiguousarray(edges[:, 0, P - 1]), "bases": v["L0_gnn_bases"],
        "w_compT": np.ascontiguousarray(v["L0_gnn_w_comp"].T), "w1": v["L1_gnn_weight"],
        "gate1T": np.ascontiguousarray(v["L1_gnn_gate_weight"][:, :, 0].T), "w2": v["L2_gnn_W"],
        "w2T": np.ascontiguousarray(v["L2_gnn_W"].T), "a_src": v["L2_gnn_a_src"], "a_dst": v["L2_gnn_a_dst"],
        "edge_wT": np.ascontiguousarray(v["L2_gnn_edge_W"].T), "edge_b": v["L2_gnn_edge_b"], "bias2": v["L2_gnn_bias"],
        "w3": v["L3_gnn_weight"], "ident_one": np.ones((1, HEADS, 1), np.float32),
    }
    nc = bacc.Bacc("TRN2", target_bir_lowering=False, num_devices=1)
    args = {k: nc.dram_tensor("in_" + k, a.shape, mybir.dt.from_np(a.dtype), kind="ExternalInput").ap() for k, a in arrays.items()}
    out = nc.dram_tensor("out_0", (N, D), F32, kind="ExternalOutput").ap()
    build(nc, out=out, **args)
    r = run_bass_kernel_spmd(nc, [{"in_" + k: np.ascontiguousarray(a) for k, a in arrays.items()}], core_ids=[0])
    return r.results[0]["out_0"]
```

```python
from contextlib import ExitStack

import concourse.bass as bass
from concourse import mybir

F32 = mybir.dt.float32
F32R = mybir.dt.float32r
I32 = mybir.dt.int32
U8 = mybir.dt.uint8
BF16 = mybir.dt.bfloat16
ALU = mybir.AluOpType
ACT = mybir.ActivationFunctionType
AX = mybir.AxisListType

P = 128
D = 256
HEADS, HD = 8, 32
HROW = HEADS * (HD + 1)
GROW = HEADS + D
W2C = D + 2 * HEADS
BASES = 8
R0, R1, R3 = 32, 16, 20
BIG = 1.0e30
EPS = 1e-5
G = 8
U = 2 * G
FIELDS = 9
DST, SRC, T32, T16, T20, NORM, ATTR = range(7)


def build(nc, x, edges, dst_last, bases, w_compT, w1, gate1T, w2, w2T, a_src, a_dst, edge_wT,
          edge_b, bias2, w3, ident_one, out, stop=None):
    N = out.shape[0]
    NWIN = x.shape[0] // P
    NW1 = -(-N // P)
    TILES = edges.shape[0]
    STEPS = TILES + NW1 - 1
    KP = -(-STEPS // U) * U
    KC = -(-KP // P)
    ITERS = KP // U
    QS = P // HEADS
    QM = KP // QS
    NSC = KP * HEADS
    BLK = 4
    assert NWIN % 2 == 0 and KP % QS == 0 and QM % BLK == 0 and KP < 256 * 4

    table = nc.dram_tensor("table", (NWIN * P, R0 * D), F32).ap()
    w0_dram = nc.dram_tensor("w0_dram", (R0, D, D), F32).ap()
    attr_dram = nc.dram_tensor("attr_dram", (KC * P, 9, P), BF16).ap()
    place_dram = nc.dram_tensor("place_dram", (KP // G, G * P), BF16).ap()
    rows_dram = nc.dram_tensor("rows_dram", (KP // G, P, G * GROW), F32).ap()
    gat_table = nc.dram_tensor("gat_table", (NWIN * P, GROW), F32).ap()

    with ExitStack() as ctx:
        def sb(name, shape, dt=F32):
            return ctx.enter_context(nc.sbuf_tensor(name, shape, dt))

        def sb_both(name, shape):
            with nc.sbuf_tensor(name, shape, F32) as plain:
                pass
            return plain, sb(name + "_r", shape, F32R)

        def sem(name):
            return ctx.enter_context(nc.semaphore(name))

        X = sb("X", [P, NWIN, D])
        A = sb("A", [P, 2 * NSC + 16])
        W, W_r = sb_both("W", [P, 2 * NSC])
        dloc = sb("dloc", [P, KP + G])
        norm = sb("norm", [P, KP + G])
        srcf = sb("srcf", [P, KP])
        types = sb("types", [P, 3, KP], U8)
        idx = sb("idx", [P, KP + U], I32)
        win = sb("win", [1, KP], U8)
        ring = sb("ring", [P, U, GROW])
        onehot = sb("onehot", [P, G, P])
        targets1 = sb("targets1", [P, G * P])
        enc = A[:, NSC + 64:NSC + 64 + 4 * HROW].rearrange("p (n e c) -> p n e c", n=2, e=2)
        prod = A[:, NSC + 1280:NSC + 1280 + 4 * HROW].rearrange("p (n e c) -> p n e c", n=2, e=2)
        work, work_r = sb_both("work", [P, 2048])
        ident = sb("ident", [P, P])
        iota = sb("iota", [P, P])
        ix = sb("ix", [P, 2, G], I32)
        stat = sb("stat", [P, 4, NWIN])
        enc_w = sb("enc_w", [96, HROW])
        enc_b = sb("enc_b", [96, HROW], BF16)
        S = sb("S", [P, G, HEADS])
        small = sb("small", [P, 32])
        gate = sb("gate", [P, 2, R1])
        col = sb("col", [P, 8])
        ps = ctx.enter_context(nc.psum_tensor("ps", [P, 8, 512], F32))

        acc = A[:, 0:NWIN * GROW].rearrange("p (w c) -> p w c", c=GROW)
        UNIT = 3 * 512
        WHALF = 12 * 2 * D
        stage = A[:, 0:4 * UNIT].rearrange("p (s c) -> p s c", s=4)
        xs = work[:, 0:512].rearrange("p (u c) -> p u c", u=2)
        xt = work[:, 512:1024].rearrange("p (u c n) -> p u c n", u=2, c=2)
        xt_high = work_r[:, 512:1024].rearrange("p (u c n) -> p u c n", u=2, c=2)
        xt_low = work_r[:, 1024:1536].rearrange("p (u c n) -> p u c n", u=2, c=2)
        attrT = work[0:96, 0:1024].bitcast(BF16).rearrange("p (h c) -> p h c", h=2)
        place = work[:, 1024:2048].bitcast(BF16).rearrange("p (h c) -> p h c", h=2)

        def w_rel(rels, low):
            return W_r[:, low * WHALF:low * WHALF + 2 * rels * D].rearrange("p (c n) -> p c n", c=2)

        alpha = A[:, 0:NSC].rearrange("p (k h) -> p k h", h=HEADS)
        hbuf = W[:, 0:NWIN * HROW].rearrange("p (w c) -> p w c", c=HROW)
        w2ext = work[:, 1024:1024 + 2 * W2C].rearrange("p (c o) -> p c o", c=2)
        gate_w = work[:, 1536:1536 + 2 * R1].rearrange("p (c r) -> p c r", c=2)
        gat_stage = A[:, 0:2 * W2C].rearrange("p (u c) -> p u c", u=2)
        w2nat = onehot[:, 0:4, :].rearrange("p (c a) b -> p c (a b)", c=2)
        gat_rows = gat_table.rearrange("(w p) c -> w p c", p=P)

        alphaT = W[:, 0:NSC]
        keyT = W[:, NSC:2 * NSC]
        maxT = W[:, NSC:2 * NSC]
        penalty = A[:, 0:NSC + 1]
        prefix = A[:, NSC + 8:2 * NSC + 8]
        ex = W[:, NSC:2 * NSC].rearrange("p (k h) -> p k h", h=HEADS)

        span = KC * P
        dl_i = A[0:NW1, 0:TILES].bitcast(I32)
        dl_f = A[0:NW1, 800:800 + TILES]
        k_i = A[0:NW1, 1600:1600 + span].bitcast(I32)
        k_f = A[0:NW1, 2500:2500 + span]
        below = A[0:NW1, 3400:3400 + span]
        junk = A[0:NW1, 4300:4300 + TILES]
        recf = A[:, 5200:5200 + KC * 5 * P].rearrange("p (k f e) -> p k f e", k=KC, f=5)
        parts = A[:, 0:KC * 9 * P // 2].bitcast(BF16).rearrange("p (k j f e) -> p k j f e", k=KC, j=3, f=3)
        rows16 = A[:, 4100:4100 + KC * P // 2].bitcast(BF16).rearrange("p (k e) -> p k e", k=KC)
        rows32 = A[:, 9700:9700 + KC * P].rearrange("p (k e) -> p k e", k=KC)
        wB = A[:, 12300:12300 + KP]
        rec = W[:, 0:KC * FIELDS * P].rearrange("p (k f e) -> p k f e", k=KC, f=FIELDS)
        w128_i = small[0:NW1, 0:1].bitcast(I32)
        w128_f = small[0:NW1, 1:2]
        below_count = small[0:NW1, 2:3]
        first_step = small[0:NW1, 3:4]
        ones_col = small[0:NW1, 16:17]
        ones_rows = onehot[0:NW1, 0, :]
        tile_f = stat[:, 0, 0:KC]
        step_f = stat[:, 1, 0:KC]
        step_i = stat[:, 2, 0:KC].bitcast(I32)
        tile_i = stat[:, 3, 0:KC].bitcast(I32)
        IB = D // 4
        HB = IB // 2
        Xflat = X[:, :, :].rearrange("p w c -> p (w c)")
        basesS = Xflat[0:4 * BASES, 0:HB * D]
        wout = Xflat[:, HB * D:HB * D + 4096].rearrange("p (s c) -> p s c", s=2)
        wsel = onehot[0:4 * BASES, 2, :]

        def rowv(n, m):
            return work[0:1, n * P:(n + m) * P]

        bar = sem("bar")
        dve_done = sem("dve_done")
        loaded = sem("loaded")
        stored = sem("stored")
        got = [sem(f"got{j}") for j in range(U)]
        claimed = sem("claimed")
        u_iota, u_ident, u_below, u_win, u_tile, u_rec, u_recf, u_turned, u_evac, u_attr, u_wsel, u_wrow, u_half, u_wps, u_wevac = (
            sem("u_" + n) for n in ("iota", "ident", "below", "win", "tile", "rec", "recf", "turned",
                                    "evac", "attr", "wsel", "wrow", "half", "wps", "wevac"))
        u_parts, u_rows = sem("u_parts"), sem("u_rows")
        u_wst = [sem(f"u_wst{s}") for s in range(2)]
        ln_var, ln_std = sem("ln_var"), sem("ln_std")
        z_zero, z_ps, z_done = sem("z_zero"), sem("z_ps"), sem("z_done")

        q_names = ("copied", "turned", "xt_high", "xt_ready", "bank_full", "bank_free", "unit_full", "gate_full", "gate_ready", "w_high")
        (q_copied, q_turned, q_xt_high, q_xt_ready, q_bank_full, q_bank_free, q_unit_full, q_gate_full, q_gate_ready,
         q_w_high) = (sem("q_" + n) for n in q_names)
        q_unit_free = [sem(f"q_unit_free{s}") for s in range(4)]
        q_w_low = sem("q_w_low")

        class Pass:
            def __init__(self, weights, rels, r0, total, gated, spare, ahead):
                self.weights, self.rels, self.r0, self.total, self.gated, self.ahead = weights, rels, r0, total, gated, ahead
                self.banks = rels * D // 512
                self.unit_banks = [range(0, -(-self.banks // 2)), range(-(-self.banks // 2), self.banks)]
                assert len(self.unit_banks[0]) * 512 <= UNIT and 2 * rels * D <= WHALF and self.banks <= (4 if gated else 6)
                self.raw = (A[:, 4 * UNIT:4 * UNIT + 2 * rels * D].rearrange("p (c n) -> p c n", c=2)
                            if spare else W[:, WHALF:WHALF + 2 * rels * D].rearrange("p (c n) -> p c n", c=2))
                self.table = table.rearrange("n c -> (n c)")[0:NWIN * P * total * D]

        class Walk:
            def __init__(self, name, nth, rels, tcol, table_):
                self.nth, self.rels, self.tcol, self.table = nth, rels, tcol, table_
                self.ix_free, self.ix_ready, self.onehot_ready, self.step_done, self.added = (
                    sem(f"{name}_{n}") for n in ("ix_free", "ix_ready", "onehot_ready", "step_done", "added"))

            def arrived(self, i):
                return i * 16 + (16 + 16 * ITERS * self.nth)

        def passes(weights, total, cuts, gated):
            made, r0 = [], total
            for n in reversed(range(len(cuts))):
                r0 -= cuts[n]
                made.insert(0, Pass(weights, cuts[n], r0, total, gated, n > 0, made[0] if made else None))
            assert r0 == 0
            return made

        p0 = passes(w0_dram, R0, (12, 10, 10), False)
        p1 = passes(w1, R1, (8, 8), True)
        p3 = passes(w3, R3, (10, 10), False)
        before = dict.fromkeys(q_names + ("unit_free",), 0)
        for p in p0 + p1 + p3:
            p.before = dict(before)
            for n, more in (("copied", NWIN), ("turned", NWIN), ("xt_high", NWIN), ("xt_ready", NWIN), ("w_high", p.banks),
                            ("bank_full", NWIN * p.banks), ("bank_free", (NWIN + 1) * p.banks), ("unit_full", 2 * NWIN),
                            ("gate_full", NWIN * p.gated), ("gate_ready", (NWIN + 2) * p.gated),
                            ("unit_free", 16 * (NWIN // 2) + 16)):
                before[n] += more
        walk0 = Walk("s0", 0, R0, 0, p0[0].table)
        walk1 = Walk("s1", 1, R1, 1, p1[0].table)
        walk3 = Walk("s3", 3, R3, 2, p3[0].table)
        gw = Walk("sg", 2, 1, 0, None)
        g_copied, g_turned, g_xt, g_out, g_row, g_hbuf = (sem("g_" + n) for n in (
            "copied", "turned", "xt", "out", "row", "hbuf"))
        g_stored = [sem(f"g_stored{u}") for u in range(2)]
        (a_targets, a_ones, a_encps, a_relu, a_hd, a_prod, a_red, a_alpha) = (
            sem("a_" + n) for n in ("targets", "ones", "encps", "relu", "hd", "prod", "red", "alpha"))
        a_attr = [sem(f"a_attr{h}") for h in range(2)]
        a_spill = [sem(f"a_spill{h}") for h in range(2)]
        m_copied, m_turned, m_evac, m_exp, m_back, m_out, m_cols, m_row = (sem("m_" + n) for n in (
            "copied", "turned", "evac", "exp", "back", "out", "cols", "row"))
        b_row = [sem(f"b_row{h}") for h in range(2)]
        b_exp, b_mult, b_onehot, b_done, b_added = (sem("b_" + n) for n in (
            "exp", "mult", "onehot", "done", "added"))

        def relational(ps_list, walk_):
            return [(part, p) for p in ps_list for part in ("split", "pass")] + [("walk", walk_)]

        PHASES = ([("setup", None), ("weights", p0[0])] + relational(p0, walk0) + [("norm", 0)] + relational(p1, walk1) +
                  [("norm", 1), ("heads", None), ("gat_rows", None), ("scores", None), ("softmax", None),
                   ("gather_sum", None), ("norm", 2)] + relational(p3, walk3) + [("norm", 3)])
        if stop is not None:
            PHASES = PHASES[:stop]

        def run(eng, parts):
            for n, (name, what) in enumerate(PHASES):
                if name in parts:
                    parts[name](what)
                eng.drain().then_inc(bar, 1)
                eng.wait_ge(bar, 5 * (n + 1))

        block = ctx.enter_context(nc.Block())

        @block.sync
        def _(sp):
            seen = [0]

            def load(dst, src):
                sp.dma_start(dst, src).then_inc(loaded, 16)
                seen[0] += 16

            def setup(_):
                load(dl_i, dst_last.partition_broadcast(NW1))
                sp.wait_ge(u_wsel, 1)
                for i4 in range(4):
                    sp.dma_start(wsel[i4 * BASES:(i4 + 1) * BASES, i4 * R0:(i4 + 1) * R0], w_compT).then_inc(u_wrow, 16)
                for half in range(2):
                    if half:
                        sp.wait_ge(u_wps, 16)
                    for i4 in range(4):
                        i0 = i4 * IB + half * HB
                        sp.dma_start(basesS[i4 * BASES:(i4 + 1) * BASES],
                                     bases[:, i0:i0 + HB, :].rearrange("b i o -> b (i o)")).then_inc(u_half, 16)
                    for n in range(4):
                        sp.wait_ge(u_wevac, 16 * half + 4 * n + 4)
                        for i4 in range(4):
                            i0 = i4 * IB + half * HB + n * 8
                            sp.dma_start(w0_dram[:, i0:i0 + 8, :].rearrange("r i o -> r (i o)"),
                                         wout[i4 * R0:(i4 + 1) * R0, n % 2, :]).then_inc(u_wst[n % 2], 16)
                for s in range(2):
                    sp.wait_ge(u_wst[s], 4 * 4 * 16)
                sp.wait_ge(u_parts, 1)
                for c in range(KC):
                    n = min(P, KP - c * P)
                    sp.dma_start(attr_dram[c * P:c * P + n].rearrange("k f e -> k (f e)"),
                                 parts[0:n, c].rearrange("p j f e -> p (j f e)")).then_inc(u_attr, 16)
                    sp.dma_start(place_dram.rearrange("g (k e) -> (g k) e", e=P)[c * P:c * P + n], rows16[0:n, c]).then_inc(u_attr, 16)
                load(X[:, :, :], x.rearrange("(w p) c -> p w c", p=P))
                sp.wait_ge(u_attr, 32 * KC)
                sp.wait_ge(loaded, seen[0])

            def load_raw(ps_):
                for c in range(2):
                    load(ps_.raw[:, c, :].rearrange("p (r o) -> p r o", o=D),
                         ps_.weights[ps_.r0:ps_.r0 + ps_.rels, c * P:(c + 1) * P, :].rearrange("r p o -> p r o"))
                if ps_.gated and ps_.r0 == 0:
                    load(gate_w[:, :, :], gate1T.rearrange("(c p) r -> p c r", p=P))

            def weights(ps_):
                load_raw(ps_)
                sp.wait_ge(loaded, seen[0])

            def store_table(ps_):
                if ps_.ahead is not None:
                    load_raw(ps_.ahead)
                rows = ps_.table.rearrange("(w p c) -> w p c", p=P, c=ps_.total * D)
                with sp.Fori(0, NWIN // 2) as i:
                    for u in range(2):
                        for v in range(2):
                            s, banks = 2 * u + v, ps_.unit_banks[v]
                            c0 = ps_.r0 * D + banks[0] * 512
                            sp.wait_ge(q_unit_full, i * 4 + (s + 1 + ps_.before["unit_full"]))
                            sp.dma_start(rows[bass.ds(i * 2 + u, 1), :, c0:c0 + len(banks) * 512].squeeze(0),
                                         stage[:, s, 0:len(banks) * 512]).then_inc(q_unit_free[s], 16)
                for s in range(4):
                    sp.wait_ge(q_unit_free[s], 16 * (NWIN // 2) + (16 + ps_.before["unit_free"]))
                sp.wait_ge(loaded, seen[0])

            def norm_loads(layer):
                if layer == 1:
                    for c in range(2):
                        load(w2ext[:, c, HEADS:HEADS + D], w2T[c * P:(c + 1) * P, :])
                        load(w2nat[:, c, :], w2[c * P:(c + 1) * P, :])
                    sp.wait_ge(z_zero, 1)
                    with nc.allow_non_contiguous_dma(reason="a few hundred words"):
                        for h in range(HEADS):
                            c, q = h // 4, h % 4
                            load(small[q * HD:(q + 1) * HD, 16 * c + h:16 * c + h + 1], a_src[h:h + 1, :].rearrange("a d -> d a"))
                            load(small[q * HD:(q + 1) * HD, 16 * c + 8 + h:16 * c + 9 + h], a_dst[h:h + 1, :].rearrange("a d -> d a"))
                        for j in range(3):
                            load(enc_w[32 * j + 9:32 * j + 10, :].rearrange("p (h d) -> p h d", d=HD + 1)[:, :, HD:HD + 1], ident_one)
                    for j in range(3):
                        for k in range(3):
                            load(enc_w[32 * j + 3 * k:32 * j + 3 * k + 3, :].rearrange("p (h d) -> p h d", d=HD + 1)[:, :, 0:HD],
                                 edge_wT.rearrange("k (h d) -> k h d", d=HD))
                        load(enc_w[32 * j + 9:32 * j + 10, :].rearrange("p (h d) -> p h d", d=HD + 1)[:, :, 0:HD],
                             edge_b.rearrange("(a h d) -> a h d", a=1, d=HD))
                if layer == 2:
                    load(ring[:, 0, 0:D], bias2.partition_broadcast(P))
                sp.wait_ge(loaded, seen[0])
                if layer == 2:
                    sp.sem_inc(z_done, 1)
                if layer in (0, 2):
                    load_raw((p1 if layer == 0 else p3)[0])
                    sp.wait_ge(loaded, seen[0])

            def store_gat_rows(_):
                with sp.Fori(0, NWIN // 2) as i:
                    for u in range(2):
                        sp.wait_ge(g_row, i * 2 + (u + 3))
                        sp.dma_start(gat_rows[bass.ds(i * 2 + u, 1)].squeeze(0), gat_stage[:, u, 0:GROW]).then_inc(g_stored[u], 16)
                for u in range(2):
                    sp.wait_ge(g_stored[u], 16 * (NWIN // 2) + 16)

            def spill(_):
                sp.wait_ge(a_ones, 1)
                with sp.Fori(0, ITERS) as i:
                    for h in range(2):
                        sp.wait_ge(a_hd, i * G + (h * G // 2 + G // 2))
                        for j in range(3):
                            sp.dma_start(attrT[32 * j:32 * j + 9, h, :].rearrange("c (k e) -> c k e", e=P),
                                         attr_dram[bass.ds(i * U + h * G, G)].rearrange("k c e -> c k e")).then_inc(a_attr[h], 16)
                        sp.dma_start(place[:, h, :], place_dram[bass.ds(i * 2 + h, 1)].squeeze(0).partition_broadcast(P)).then_inc(a_attr[h], 16)
                    for h in range(2):
                        for j in range(G):
                            sp.wait_ge(got[h * G + j], gw.arrived(i))
                        sp.dma_start(rows_dram[bass.ds(i * 2 + h, 1)].squeeze(0),
                                     ring[:, h * G:(h + 1) * G, :].rearrange("p s c -> p (s c)")).then_inc(a_spill[h], 16)
                for h in range(2):
                    sp.wait_ge(a_spill[h], 16 * ITERS + 16)

            def reload(_):
                with sp.Fori(0, ITERS) as i:
                    for h in range(2):
                        sp.wait_ge(b_done, i * U + (h * G + G))
                        sp.dma_start(ring[:, h * G:(h + 1) * G, :].rearrange("p s c -> p (s c)"),
                                     rows_dram[bass.ds(i * 2 + h, 1)].squeeze(0)).then_inc(b_row[h], 16)

            run(sp, {"setup": setup, "weights": weights, "pass": store_table, "norm": norm_loads,
                     "gat_rows": store_gat_rows, "scores": spill, "gather_sum": reload})
            full = N // P
            sp.dma_start(out[0:full * P, :].rearrange("(w p) c -> p w c", p=P), X[:, 0:full, :]).then_inc(stored, 16)
            sp.dma_start(out[full * P:N, :], X[0:N - full * P, full, :]).then_inc(stored, 16)
            sp.wait_ge(stored, 32)

        @block.gpsimd
        def _(pool):
            def setup(_):
                pool.iota(w128_i, [[0, 1]], base=0, channel_multiplier=P).then_inc(u_iota, 1)
                pool.iota(k_i, [[1, span]], base=0, channel_multiplier=0).then_inc(u_iota, 1)
                pool.iota(step_i, [[P, KC]], base=0, channel_multiplier=1).then_inc(u_iota, 1)
                pool.iota(iota[:, :], [[1, P]], base=0, channel_multiplier=0,
                          allow_small_or_imprecise_dtypes=True).then_inc(u_iota, 1)
                pool.iota(col[:, 7:8], [[0, 1]], base=0, channel_multiplier=1,
                          allow_small_or_imprecise_dtypes=True).then_inc(u_iota, 1)
                pool.memset(ident[:, :], 0.0).then_inc(u_ident, 1)
                pool.wait_ge(u_ident, 1)
                pool.affine_select(out=ident[:, :], in_=ident[:, :], compare_op=ALU.not_equal, fill=1.0,
                                   base=0, pattern=[[-1, P]], channel_multiplier=1).then_inc(u_ident, 1)
                pool.wait_ge(u_tile, 1)
                for c in range(KC):
                    pool.indirect_dma_start(out=rec[:, c, :, :].rearrange("p f e -> p (f e)").bitcast(I32), out_offset=None,
                                            in_=edges.rearrange("t f e -> t (f e)"),
                                            in_offset=bass.IndirectOffsetOnAxis(ap=tile_i[:, c:c + 1], axis=0)).then_inc(u_rec, 16)
                pool.wait_ge(u_rec, 16 * KC)

            def gather(src, width, wk, spilled=None):
                with pool.Fori(0, ITERS) as i:
                    for h in range(2):
                        pool.wait_ge(wk.ix_ready, i * 2 + (h + 1))
                        if spilled is not None:
                            pool.wait_ge(spilled[h], i * 16 + 16)
                        pool.sem_inc(claimed, 1)
                        for j in range(G):
                            pool.indirect_dma_start(out=ring[:, h * G + j, 0:width], out_offset=None, in_=src,
                                                    in_offset=bass.IndirectOffsetOnAxis(ap=ix[:, h, j:j + 1], axis=0)
                                                    ).then_inc(got[h * G + j], 16)

            def walk(wk):
                gather(wk.table.rearrange("(a o) -> a o", o=D), D, wk)

            def scores(_):
                gather(gat_table, GROW, gw, a_spill)

            def weigh(_):
                with pool.Fori(0, ITERS) as i:
                    for h in range(2):
                        half = ring[:, h * G:(h + 1) * G, :]
                        rows = half[:, :, HEADS:GROW].rearrange("p k (h d) -> p k h d", d=HD)
                        pool.wait_ge(b_exp, i * 2 + (h + 1))
                        pool.tensor_tensor(rows, rows, half[:, :, 0:HEADS].unsqueeze(3).to_broadcast([P, G, HEADS, HD]),
                                           ALU.mult).then_inc(b_mult, 1)

            run(pool, {"setup": setup, "walk": walk, "scores": scores, "gather_sum": weigh})

        @block.vector
        def _(dve):
            done = [0]

            def ch(ins):
                ins.then_inc(dve_done, 1)
                done[0] += 1
                dve.wait_ge(dve_done, done[0])

            def setup(_):
                ch(dve.memset(wsel, 0.0))
                dve.sem_inc(u_wsel, 1)
                ch(dve.memset(ones_rows, 1.0))
                ch(dve.memset(ones_col, 1.0))
                dve.wait_ge(u_iota, 5)
                dve.wait_ge(loaded, 16)
                ch(dve.tensor_copy(dl_f, dl_i))
                ch(dve.tensor_copy(w128_f, w128_i))
                ch(dve.tensor_copy(k_f, k_i))
                ch(dve.tensor_scalar(junk, dl_f, w128_f, 0.0, ALU.is_lt, ALU.add, accum_out=below_count))
                ch(dve.scalar_tensor_tensor(first_step, w128_f, 1.0 / P, below_count, ALU.mult, ALU.add))
                ch(dve.tensor_scalar(below, k_f, first_step, None, ALU.is_ge))
                dve.sem_inc(u_below, 1)
                dve.wait_ge(u_win, 1)
                for c in range(2):
                    n = min(span // 2, KP - c * (span // 2))
                    ch(dve.tensor_scalar(wB[:, c * (span // 2):c * (span // 2) + n], ps[:, c, 0:n], -1.0, None, ALU.add))
                ch(dve.tensor_copy(win[0:1, :], wB[0:1, :]))
                ch(dve.tensor_copy(step_f, step_i))
                ch(dve.scalar_tensor_tensor(tile_f, ps[:, 2, 0:KC], -1.0, step_f, ALU.mult, ALU.add))
                ch(dve.tensor_scalar(tile_i, tile_f, 1.0, float(TILES - 1), ALU.add, ALU.min))
                dve.sem_inc(u_tile, 1)
                dve.wait_ge(u_rec, 16 * KC)
                ch(dve.tensor_copy(recf, rec[:, :, 0:5, :].bitcast(I32)))
                dve.sem_inc(u_recf, 1)
                dest = [dloc, srcf, types[:, 0, :], types[:, 1, :], types[:, 2, :], norm]
                for f in range(6):
                    for c in range(KC):
                        m, n = f * KC + c, min(P, KP - c * P)
                        dve.wait_ge(u_turned, m + 1)
                        dve.tensor_copy(dest[f][:, c * P:c * P + n], ps[:, 3 + m % 3, 0:n]).then_inc(u_evac, 1)
                dve.wait_ge(u_evac, 6 * KC)
                attrs = rec[:, :, ATTR:ATTR + 3, :]
                for n in range(3):
                    ch(dve.tensor_copy(parts[:, :, n], attrs))
                    if n < 2:
                        ch(dve.tensor_tensor(attrs, attrs, parts[:, :, n], ALU.subtract))
                ch(dve.tensor_scalar(tile_f, ps[:, 2, 0:KC], -1.0, float(P), ALU.add, ALU.mult))
                for c in range(KC):
                    dve.tensor_scalar(rows32[:, c], recf[:, c, DST, :], tile_f[:, c:c + 1], -1.0, ALU.subtract, ALU.max).then_inc(u_rows, 1)
                dve.wait_ge(u_rows, KC)
                ch(dve.tensor_scalar(rows16, rows32, float(P), None, ALU.min))
                dve.sem_inc(u_parts, 1)
                ch(dve.scalar_tensor_tensor(dloc[:, 0:KP], wB, -float(P), dloc[:, 0:KP], ALU.mult, ALU.add))
                ch(dve.memset(dloc[:, STEPS:KP + G], -1.0))
                ch(dve.memset(norm[:, KP:KP + G], 0.0))
                ch(dve.memset(idx[:, KP:KP + U], 0.0))

            def split(ps_):
                for b in range(ps_.banks):
                    bank = slice(b * 512, (b + 1) * 512)
                    low = w_rel(ps_.rels, 1)[:, :, bank]
                    dve.wait_ge(q_w_high, b + (1 + ps_.before["w_high"]))
                    dve.tensor_tensor(low, ps_.raw[:, :, bank], w_rel(ps_.rels, 0)[:, :, bank].bitcast(F32), ALU.subtract).then_inc(q_w_low, 1)

            def copies(ps_):
                def to_place(window, u):
                    dve.tensor_copy(xs[:, u, :], X[:, bass.ds(window, 1), :].squeeze(1)).then_inc(q_copied, 1)

                def body(i, more):
                    for u in range(2):
                        turned = ps[:, 6 + u, 0:D].rearrange("p (c n) -> p c n", c=2)
                        dve.wait_ge(q_turned, i * 2 + (u + 1 + ps_.before["turned"]))
                        dve.tensor_copy(xt_high[:, u, :, :], turned).then_inc(q_xt_high, 1)
                        if more:
                            to_place(i * 2 + (u + 2), u)
                        dve.wait_ge(q_xt_high, i * 2 + (u + 1 + ps_.before["xt_high"]))
                        dve.tensor_tensor(xt_low[:, u, :, :], turned, xt_high[:, u, :, :].bitcast(F32), ALU.subtract).then_inc(q_xt_ready, 1)

                for u in range(2):
                    dve.tensor_copy(xs[:, u, :], X[:, u, :]).then_inc(q_copied, 1)
                with dve.Fori(0, NWIN // 2 - 1) as i:
                    body(i, True)
                body(NWIN // 2 - 1, False)

            def window_registers(i, h):
                _, regs = nc.values_load_multi_w_load_instructions(
                    win[0:1, bass.ds(i * U + h * G, G)], engines=[dve.engine], min_val=0, max_val=NWIN - 1,
                    skip_runtime_bounds_check_because="a step's window counts windows that have begun, at most all of them")
                return regs

            def steps(width, weighed, onehot_ready, step_done, added):
                def build(s, j):
                    dve.tensor_scalar(onehot[:, j, :], iota[:, :], dloc[:, s], norm[:, s] if weighed else None, ALU.is_equal,
                                      ALU.mult if weighed else ALU.bypass).then_inc(onehot_ready, 1)

                for j in range(G):
                    build(slice(j, j + 1), j)
                with dve.Fori(0, ITERS) as i:
                    for h in range(2):
                        regs = window_registers(i, h)
                        for j in range(G):
                            dve.wait_ge(step_done, i * U + (h * G + j + 1 + U))
                            build(bass.ds(i * U + (h * G + j + G), 1), j)
                            dve.wait_ge(added, i * U + (h * G + j + G))
                            a = acc[:, bass.ds(regs[j], 1), 0:width].squeeze(1)
                            dve.tensor_tensor(a, a, ps[:, j, 0:width], ALU.add).then_inc(added, 1)
                dve.wait_ge(added, KP + G)
                dve.wait_ge(onehot_ready, KP + G)

            def walk(wk):
                ch(dve.scalar_tensor_tensor(idx[:, 0:KP], srcf[:, :], float(wk.rels), types[:, wk.tcol, :], ALU.mult, ALU.add))
                ch(dve.memset(A[:, 0:NWIN * GROW], 0.0))
                dve.sem_inc(wk.ix_free, 1)
                dve.sem_inc(wk.added, G)
                steps(D, True, wk.onehot_ready, wk.step_done, wk.added)

            def residual_norm(layer):
                mean, var, rstd = stat[:, 0, :], stat[:, 1, :], stat[:, 2, :]
                if layer == 1:
                    ch(dve.memset(small[:, :], 0.0))
                    ch(dve.memset(enc_w[:, :], 0.0))
                    dve.sem_inc(z_zero, 1)
                if layer == 2:
                    a = acc[:, :, HEADS:GROW]
                    ch(dve.tensor_scalar(acc[:, :, 0:HEADS], acc[:, :, 0:HEADS], 1e-10, None, ALU.max))
                    ch(dve.reciprocal(acc[:, :, 0:HEADS], acc[:, :, 0:HEADS]))
                    ah = a.rearrange("p w (h d) -> p w h d", d=HD)
                    ch(dve.tensor_tensor(ah, ah, acc[:, :, 0:HEADS].unsqueeze(3).to_broadcast([P, NWIN, HEADS, HD]), ALU.mult))
                    dve.wait_ge(z_done, 1)
                    ch(dve.tensor_tensor(a, a, ring[:, 0:1, 0:D].to_broadcast([P, NWIN, D]), ALU.add))
                    ch(dve.tensor_tensor(X[:, :, :], a, X[:, :, :], ALU.add))
                else:
                    ch(dve.scalar_tensor_tensor(X[:, :, :], acc[:, :, 0:D], 0.0, X[:, :, :], ALU.max, ALU.add))
                ch(dve.tensor_reduce(mean, X[:, :, :], AX.X, ALU.add))
                ch(dve.tensor_scalar(mean, mean, 1.0 / D, None, ALU.mult))
                ch(dve.tensor_tensor(X[:, :, :], X[:, :, :], mean.unsqueeze(2).to_broadcast([P, NWIN, D]), ALU.subtract))
                ch(dve.tensor_tensor(acc[:, :, 0:D], X[:, :, :], X[:, :, :], ALU.mult))
                ch(dve.tensor_reduce(var, acc[:, :, 0:D], AX.X, ALU.add))
                ch(dve.tensor_scalar(var, var, 1.0 / D, EPS, ALU.mult, ALU.add))
                dve.sem_inc(ln_var, 1)
                dve.wait_ge(ln_std, layer + 1)
                ch(dve.reciprocal(rstd, rstd))
                ch(dve.tensor_tensor(X[:, :, :], X[:, :, :], rstd.unsqueeze(2).to_broadcast([P, NWIN, D]), ALU.mult))

            def heads(_):
                part, rest = A[0:96, 0:HROW // 2].bitcast(BF16), A[0:96, 512:512 + HROW]
                ch(dve.tensor_copy(part, enc_w[:, :]))
                ch(dve.tensor_copy(enc_b[0:32, :], part[0:32]))
                ch(dve.tensor_tensor(rest, enc_w[:, :], part, ALU.subtract))
                ch(dve.tensor_copy(part, rest))
                ch(dve.tensor_copy(enc_b[32:64, :], part[32:64]))
                ch(dve.tensor_tensor(rest, rest, part, ALU.subtract))
                ch(dve.tensor_copy(enc_b[64:96, :], rest[64:96]))
                for c in range(2):
                    dve.wait_ge(z_ps, c + 1)
                    ch(dve.tensor_copy(w2ext[:, c, 0:HEADS], ps[:, c, 0:HEADS]))
                    ch(dve.tensor_copy(w2ext[:, c, HEADS + D:W2C], ps[:, c, HEADS:2 * HEADS]))

            def gat_rows_(_):
                dve.sem_inc(g_hbuf, 2)
                with dve.Fori(0, NWIN // 2) as i:
                    for u in range(2):
                        dve.tensor_copy(xs[:, u, :], X[:, bass.ds(i * 2 + u, 1), :].squeeze(1)).then_inc(g_copied, 1)
                    for u in range(2):
                        dve.wait_ge(g_turned, i * 2 + (u + 1))
                        dve.tensor_copy(xt[:, u, :, :], ps[:, 6 + u, 0:D].rearrange("p (c n) -> p c n", c=2)).then_inc(g_xt, 1)
                    for u in range(2):
                        dve.wait_ge(g_row, i * 2 + (u + 3))
                        row = hbuf[:, bass.ds(i * 2 + u, 1), :].squeeze(1).rearrange("p (h d) -> p h d", d=HD + 1)
                        dve.tensor_copy(row[:, :, 0:HD], gat_stage[:, u, HEADS:HEADS + D].rearrange("p (h d) -> p h d", d=HD))
                        dve.tensor_copy(row[:, :, HD:HD + 1], gat_stage[:, u, HEADS + D:W2C].unsqueeze(2)).then_inc(g_hbuf, 1)

            def scores(_):
                ch(dve.tensor_copy(idx[:, 0:KP], srcf[:, :]))
                for h in range(2):
                    dve.tensor_copy(ix[:, h, :], idx[:, h * G:(h + 1) * G]).then_inc(gw.ix_ready, 1)
                ch(dve.memset(attrT[:, :, :], 0.0))
                for j in range(3):
                    ch(dve.memset(attrT[32 * j:32 * j + 10, :, :], 1.0))
                dve.sem_inc(a_ones, 1)
                dve.sem_inc(a_prod, 2)
                dve.sem_inc(a_red, 2)
                dve.sem_inc(a_alpha, 1)
                targets = [onehot[:, :, :].rearrange("p k e -> p (k e)"), targets1[:, :]]
                with dve.Fori(0, ITERS) as i:
                    for h in range(2):
                        dve.wait_ge(a_attr[h], i * 64 + 64)
                        dve.tensor_scalar(targets[h], place[:, h, :], col[:, 7:8], None, ALU.is_equal).then_inc(a_targets, 1)

                        def reduce_pair(n, q):
                            dve.wait_ge(a_prod, n + 3)
                            if q == 0:
                                dve.wait_ge(a_alpha, i * 2 + (h + 1))
                            dve.tensor_reduce(S[:, 2 * q:2 * q + 2, :], prod[:, q % 2].rearrange("p e (h d) -> p e h d", d=HD + 1),
                                              AX.X, ALU.add).then_inc(a_red, 1)

                        for q in range(4):
                            n = i * G + (h * 4 + q)
                            dve.wait_ge(a_hd, n + (1 + G))
                            dve.wait_ge(a_relu, n + 3)
                            dve.wait_ge(a_red, n + 1)
                            dve.tensor_tensor(prod[:, q % 2], enc[:, q % 2], ps[:, 4 + 2 * (q % 2):6 + 2 * (q % 2), 0:HROW],
                                              ALU.mult).then_inc(a_prod, 1)
                            if q:
                                reduce_pair(i * G + (h * 4 + q - 1), q - 1)
                        reduce_pair(i * G + (h * 4 + 3), 3)
                        dve.wait_ge(a_red, i * G + (h * 4 + 4 + 2))
                        for j in range(G):
                            dve.wait_ge(got[h * G + j], gw.arrived(i))
                        dve.tensor_tensor(alpha[:, bass.ds(i * U + h * G, G), :], S[:, :, :],
                                          ring[:, h * G:(h + 1) * G, 0:HEADS], ALU.add).then_inc(a_alpha, 1)
                        dve.wait_ge(a_alpha, i * 2 + (h + 2))
                        dve.tensor_copy(ix[:, h, :], idx[:, bass.ds(i * U + (h * G + U), G)]).then_inc(gw.ix_ready, 1)
                dve.wait_ge(gw.ix_ready, 2 * ITERS + 2)

            def softmax(_):
                ch(dve.scalar_tensor_tensor(A[:, 0:NSC], A[:, 0:NSC], 0.2, A[:, 0:NSC], ALU.mult, ALU.max))
                dve.sem_inc(m_turned, 1)
                av = A[:, 0:NSC].rearrange("p (q m h) -> p q m h", q=QS, h=HEADS)
                dv = dloc[:, 0:KP].rearrange("p (q m) -> p q m", q=QS)
                with dve.Fori(0, QM // BLK) as i:
                    dve.wait_ge(m_turned, i + 1)
                    for b in range(BLK):
                        dst = work[:, b * P:(b + 1) * P].rearrange("p (q h) -> p q h", h=HEADS)
                        key = work[:, 512 + b * P:512 + (b + 1) * P].rearrange("p (q h) -> p q h", h=HEADS)
                        dve.tensor_copy(dst, av[:, :, bass.ds(i * BLK + b, 1), :].squeeze(2))
                        ins = dve.tensor_copy(key, dv[:, :, bass.ds(i * BLK + b, 1)].to_broadcast([P, QS, HEADS]))
                    ins.then_inc(m_copied, 1)
                dve.wait_ge(m_evac, 2 * (QM // BLK) + 2)
                ch(dve.tensor_tensor(penalty[:, 1:NSC], keyT[:, 1:NSC], keyT[:, 0:NSC - 1], ALU.not_equal))
                ch(dve.tensor_scalar(penalty[:, 1:NSC], penalty[:, 1:NSC], -BIG, None, ALU.mult))
                ch(dve.tensor_reduce(col[:, 0:1], penalty[:, 1:NSC], AX.X, ALU.min))
                ch(dve.tensor_copy(col[:, 1:2], keyT[:, 0:1]))
                ch(dve.tensor_copy(col[:, 2:3], keyT[:, NSC - 1:NSC]))
                ch(dve.memset(penalty[:, 0:1], -BIG))
                ch(dve.tensor_tensor_scan(prefix, penalty[:, 0:NSC], alphaT, -BIG, ALU.add, ALU.max))
                ch(dve.tensor_copy(col[:, 3:4], prefix[:, NSC - 1:NSC]))
                dve.sem_inc(m_cols, 1)
                dve.wait_ge(m_row, 1)
                ch(dve.tensor_copy(rowv(0, 4), ps[0:1, 0, 0:4 * P]))
                whole, fk, lk, tail, link, nlink, pen_q, car = (rowv(n, 1) for n in range(8))
                H8 = HEADS
                ch(dve.memset(link, 0.0))
                ch(dve.tensor_tensor(link[:, H8:P], fk[:, H8:P], lk[:, 0:P - H8], ALU.is_equal))
                ch(dve.tensor_scalar(link, link, -1.0, BIG, ALU.add, ALU.mult))
                ch(dve.memset(nlink, -BIG))
                ch(dve.tensor_copy(nlink[:, 0:P - H8], link[:, H8:P]))
                by_head = "o (q h) -> o h q"
                a_hq, b_hq, c_hq = (rowv(n, 1) for n in (8, 9, 10))
                hq = "o (h q) -> o h q"

                def carries(lnk, ends, rev, out_row):
                    ch(dve.tensor_tensor(pen_q, lnk, whole, ALU.add))
                    for src_, dst_ in ((pen_q, a_hq), (ends, b_hq)):
                        v = src_.rearrange(by_head, h=HEADS)
                        v = v[:, :, ::-1] if rev else v
                        ch(dve.tensor_copy(dst_.rearrange(hq, h=HEADS), v))
                    ch(dve.tensor_tensor_scan(c_hq, a_hq, b_hq, -BIG, ALU.add, ALU.max))
                    ch(dve.memset(out_row, -BIG))
                    o = out_row.rearrange(by_head, h=HEADS)
                    cv = c_hq.rearrange(hq, h=HEADS)
                    if rev:
                        ch(dve.tensor_copy(o[:, :, 0:QS - 1], cv[:, :, 0:QS - 1][:, :, ::-1]))
                    else:
                        ch(dve.tensor_copy(o[:, :, 1:QS], cv[:, :, 0:QS - 1]))

                carries(link, tail, False, car)
                dve.sem_inc(m_cols, 1)
                dve.wait_ge(m_row, 2)
                ch(dve.tensor_copy(col[:, 4:7], ps[:, 1, 0:3]))
                ch(dve.tensor_copy(penalty[:, 0:1], col[:, 4:5]))
                ch(dve.tensor_copy(penalty[:, NSC:NSC + 1], col[:, 5:6]))
                ch(dve.tensor_tensor_scan(prefix, penalty[:, 0:NSC], alphaT, col[:, 6:7], ALU.add, ALU.max))
                ch(dve.tensor_tensor_scan(maxT[:, ::-1], penalty[:, 1:NSC + 1][:, ::-1], prefix[:, ::-1], -BIG, ALU.add, ALU.max))
                ch(dve.tensor_copy(col[:, 3:4], maxT[:, 0:1]))
                dve.sem_inc(m_cols, 1)
                dve.wait_ge(m_row, 3)
                ch(dve.tensor_copy(tail, ps[0:1, 0, 0:P]))
                carries(nlink, tail, True, car)
                dve.sem_inc(m_cols, 1)
                dve.wait_ge(m_row, 4)
                ch(dve.tensor_copy(col[:, 6:7], ps[:, 1, 0:1]))
                ch(dve.tensor_tensor_scan(maxT[:, ::-1], penalty[:, 1:NSC + 1][:, ::-1], prefix[:, ::-1], col[:, 6:7], ALU.add, ALU.max))
                ch(dve.tensor_tensor(alphaT, alphaT, maxT, ALU.subtract))
                dve.sem_inc(m_back, 1)
                dve.sem_inc(m_out, 1)
                exq = W[:, NSC:2 * NSC].rearrange("p (q m h) -> p q m h", q=QS, h=HEADS)
                with dve.Fori(0, QM // BLK) as i:
                    dve.wait_ge(m_back, i + 2)
                    for b in range(BLK):
                        ins = dve.tensor_copy(exq[:, :, bass.ds(i * BLK + b, 1), :].squeeze(2),
                                              ps[:, 2, b * P:(b + 1) * P].rearrange("p (q h) -> p q h", h=HEADS))
                    ins.then_inc(m_out, 1)
                ch(dve.memset(A[:, 0:NWIN * GROW], 0.0))

            def gather_sum(_):
                dve.sem_inc(b_added, G)
                steps(GROW, False, b_onehot, b_done, b_added)

            run(dve, {"setup": setup, "split": split, "pass": copies, "walk": walk, "norm": residual_norm, "heads": heads,
                      "gat_rows": gat_rows_, "scores": scores, "softmax": softmax, "gather_sum": gather_sum})

        @block.scalar
        def _(act):
            def setup(_):
                for m in range(32):
                    n = m // 4
                    act.wait_ge(u_wps, m + 1)
                    if m % 4 == 0 and n >= 2:
                        act.wait_ge(u_wst[n % 2], 64 * (n // 2))
                    act.activation(wout[:, n % 2, (m % 4) * 512:(m % 4 + 1) * 512], ps[:, 6 + m % 2, :], ACT.Copy).then_inc(u_wevac, 1)

            def split(ps_):
                for b in range(ps_.banks):
                    bank = slice(b * 512, (b + 1) * 512)
                    act.activation(w_rel(ps_.rels, 0)[:, :, bank], ps_.raw[:, :, bank], ACT.Copy).then_inc(q_w_high, 1)

            def evacuate(ps_):
                act.sem_inc(q_bank_free, ps_.banks)
                if ps_.gated:
                    act.sem_inc(q_gate_ready, 2)
                for s in range(4):
                    act.sem_inc(q_unit_free[s], 16)
                with act.Fori(0, NWIN // 2) as i:
                    for u in range(2):
                        if ps_.gated:
                            act.wait_ge(q_gate_full, i * 2 + (u + 1 + ps_.before["gate_full"]))
                            act.activation(gate[:, u, :], ps[:, 4 + u, 0:R1], ACT.Sigmoid).then_inc(q_gate_ready, 1)
                            act.wait_ge(q_gate_ready, i * 2 + (u + 3 + ps_.before["gate_ready"]))
                        for v in range(2):
                            s = 2 * u + v
                            act.wait_ge(q_unit_free[s], i * 16 + (16 + ps_.before["unit_free"]))
                            for k, b in enumerate(ps_.unit_banks[v]):
                                dst = stage[:, s, k * 512:(k + 1) * 512]
                                act.wait_ge(q_bank_full, i * (2 * ps_.banks) + (u * ps_.banks + b + 1 + ps_.before["bank_full"]))
                                if ps_.gated:
                                    r = ps_.r0 + 2 * b
                                    act.activation(dst[:, 0:D], ps[:, b, 0:D], ACT.Copy, scale=gate[:, u, r:r + 1])
                                    ins = act.activation(dst[:, D:512], ps[:, b, D:512], ACT.Copy, scale=gate[:, u, r + 1:r + 2])
                                else:
                                    ins = act.activation(dst, ps[:, b, :], ACT.Copy)
                                ins.then_inc(q_bank_free, 1)
                            act.wait_ge(q_bank_free, i * (2 * ps_.banks) + ((u + 1) * ps_.banks + ps_.unit_banks[v][-1] + 1 + ps_.before["bank_free"]))
                            act.sem_inc(q_unit_full, 1)

            def indices(wk):
                act.wait_ge(wk.ix_free, 1)
                with act.Fori(0, ITERS) as i:
                    for h in range(2):
                        act.wait_ge(wk.step_done, i * U + (h * G + G))
                        act.activation(ix[:, h, :], idx[:, bass.ds(i * U + h * G, G)], ACT.Copy).then_inc(wk.ix_ready, 1)

            def std(layer):
                act.wait_ge(ln_var, layer + 1)
                act.activation(stat[:, 2, :], stat[:, 1, :], ACT.Sqrt).then_inc(ln_std, 1)

            def gat_rows_(_):
                act.sem_inc(g_row, 2)
                for u in range(2):
                    act.sem_inc(g_stored[u], 16)
                with act.Fori(0, NWIN // 2) as i:
                    for u in range(2):
                        act.wait_ge(g_out, i * 2 + (u + 1))
                        act.wait_ge(g_stored[u], i * 16 + 16)
                        act.wait_ge(g_hbuf, i * 2 + (u + 1))
                        act.activation(gat_stage[:, u, :], ps[:, u, 0:W2C], ACT.Copy).then_inc(g_row, 1)

            def scores(_):
                act.sem_inc(a_relu, 2)
                for h in range(2):
                    act.sem_inc(a_spill[h], 16)
                with act.Fori(0, ITERS) as i:
                    for q in range(G):
                        n, e = i * G + q, q % 2
                        act.wait_ge(a_encps, n + 1)
                        act.wait_ge(a_prod, n + 1)
                        act.activation(enc[:, e], ps[:, 2 * e:2 * e + 2, 0:HROW], ACT.Relu).then_inc(a_relu, 1)

            def softmax(_):
                act.sem_inc(m_evac, 2)
                with act.Fori(0, QM // BLK) as i:
                    act.wait_ge(m_turned, i + 2)
                    act.activation(W[:, bass.ds(i * 512, 512)], ps[:, 0, :], ACT.Copy).then_inc(m_evac, 1)
                    act.activation(W[:, bass.ds(i * 512 + NSC, 512)], ps[:, 1, :], ACT.Copy).then_inc(m_evac, 1)
                with act.Fori(0, QM // BLK) as i:
                    act.wait_ge(m_back, i + 1)
                    act.activation(work[:, 0:512], W[:, bass.ds(i * 512, 512)], ACT.Exp).then_inc(m_exp, 1)

            def exps(_):
                with act.Fori(0, ITERS) as i:
                    for h in range(2):
                        act.wait_ge(b_row[h], i * 16 + 16)
                        act.activation(ring[:, h * G:(h + 1) * G, 0:HEADS], ex[:, bass.ds(i * U + h * G, G), :], ACT.Copy).then_inc(b_exp, 1)

            run(act, {"setup": setup, "split": split, "pass": evacuate, "walk": indices, "norm": std, "gat_rows": gat_rows_,
                      "scores": scores, "softmax": softmax, "gather_sum": exps})

        @block.tensor
        def _(pe):
            def setup(_):
                pe.wait_ge(u_below, 1)
                for c in range(2):
                    pe.matmul(ps[:, c, 0:span // 2], ones_rows, below[:, c * (span // 2):(c + 1) * (span // 2)], start=True, stop=True)
                for c in range(KC):
                    ins = pe.matmul(ps[:, 2, c:c + 1], below[:, c * P:(c + 1) * P], ones_col, start=True, stop=True)
                ins.then_inc(u_win, 1)
                pe.wait_ge(u_wrow, 64)
                for m in range(32):
                    if m % 16 == 0:
                        pe.wait_ge(u_half, 64 * (m // 16 + 1))
                    if m >= 2:
                        pe.wait_ge(u_wevac, m - 1)
                    pe.matmul(ps[:, 6 + m % 2, :], wsel, basesS[:, (m % 16) * 512:(m % 16 + 1) * 512], start=True, stop=True).then_inc(u_wps, 1)
                pe.wait_ge(u_recf, 1)
                pe.wait_ge(u_ident, 2)
                for f in range(6):
                    for c in range(KC):
                        m = f * KC + c
                        if m >= 3:
                            pe.wait_ge(u_evac, m - 2)
                        pe.transpose(ps[:, 3 + m % 3, 0:P], recf[:, c, f, :] if f < 5 else rec[:, c, NORM, :], ident[:, :]).then_inc(u_turned, 1)

            def turn(i, copied, turned_):
                for u in range(2):
                    pe.wait_ge(copied, i * 2 + (u + 1))
                    for c in range(2):
                        ins = pe.transpose(ps[:, 6 + u, c * P:(c + 1) * P], xs[:, u, c * P:(c + 1) * P], ident[:, :])
                    ins.then_inc(turned_, 1)

            def products(ps_):
                high, low = w_rel(ps_.rels, 0), w_rel(ps_.rels, 1)

                def turn_window(n, u):
                    pe.wait_ge(q_copied, n + (1 + ps_.before["copied"]))
                    for c in range(2):
                        ins = pe.transpose(ps[:, 6 + u, c * P:(c + 1) * P], xs[:, u, c * P:(c + 1) * P], ident[:, :])
                    ins.then_inc(q_turned, 1)

                def body(i, more):
                    for u in range(2):
                        pe.wait_ge(q_xt_ready, i * 2 + (u + 1 + ps_.before["xt_ready"]))
                        if ps_.gated:
                            pe.wait_ge(q_gate_ready, i * 2 + (u + 1 + ps_.before["gate_ready"]))
                            for n in range(4):
                                ins = pe.matmul(ps[:, 4 + u, 0:R1], (xt_high, xt_low)[n // 2][:, u, n % 2, :].bitcast(F32), gate_w[:, n % 2, :],
                                                start=(n == 0), stop=(n == 3))
                            ins.then_inc(q_gate_full, 1)
                        for b in range(ps_.banks):
                            pe.wait_ge(q_bank_free, i * (2 * ps_.banks) + (u * ps_.banks + b + 1 + ps_.before["bank_free"]))
                            terms = [(xt_high, high, c) for c in range(2)] + [(xt_high, low, c) for c in range(2)] + [(xt_low, high, c) for c in range(2)]
                            for n, (rows, w, c) in enumerate(terms):
                                ins = pe.matmul(ps[:, b, :], rows[:, u, c, :], w[:, c, b * 512:(b + 1) * 512],
                                                start=(n == 0), stop=(n == len(terms) - 1))
                            ins.then_inc(q_bank_full, 1)
                        if more:
                            turn_window(i * 2 + (u + 2), u)

                for u in range(2):
                    turn_window(u, u)
                with pe.Fori(0, NWIN // 2 - 1) as i:
                    body(i, True)
                body(NWIN // 2 - 1, False)

            def walk(wk):
                pe.sem_inc(wk.step_done, U)
                with pe.Fori(0, ITERS) as i:
                    for h in range(2):
                        for j in range(G):
                            s = i * U + (h * G + j)
                            pe.wait_ge(got[h * G + j], wk.arrived(i))
                            pe.wait_ge(wk.onehot_ready, s + 1)
                            pe.wait_ge(wk.added, s + 1)
                            pe.matmul(ps[:, j, 0:D], onehot[:, j, :], ring[:, h * G + j, 0:D], start=True, stop=True).then_inc(wk.step_done, 1)

            def heads(_):
                for c in range(2):
                    for k in range(2):
                        ins = pe.matmul(ps[:, c, 0:2 * HEADS], w2nat[:, k, c * P:(c + 1) * P], small[:, 16 * k:16 * k + 16],
                                        start=(k == 0), stop=(k == 1))
                    ins.then_inc(z_ps, 1)

            def gat_rows_(_):
                with pe.Fori(0, NWIN // 2) as i:
                    turn(i, g_copied, g_turned)
                    for u in range(2):
                        pe.wait_ge(g_xt, i * 2 + (u + 1))
                        pe.wait_ge(g_row, i * 2 + (u + 1))
                        for c in range(2):
                            ins = pe.matmul(ps[:, u, 0:W2C], xt[:, u, c, :], w2ext[:, c, :], start=(c == 0), stop=(c == 1))
                        ins.then_inc(g_out, 1)

            def scores(_):
                pe.sem_inc(a_hd, G)
                targets = [onehot, targets1[:, :].rearrange("p (k e) -> p k e", e=P)]
                with pe.Fori(0, ITERS) as i:
                    for h in range(2):
                        _, regs = nc.values_load_multi_w_load_instructions(
                            win[0:1, bass.ds(i * U + h * G, G)], engines=[pe.engine], min_val=0, max_val=NWIN - 1,
                            skip_runtime_bounds_check_because="a step's window counts windows that have begun, at most all of them")
                        pe.wait_ge(a_attr[h], i * 64 + 64)
                        for q in range(4):
                            n, e = i * G + (h * 4 + q), q % 2
                            pe.wait_ge(a_relu, n + 1)
                            for k in range(2):
                                j = 2 * q + k
                                ins = pe.matmul(ps[:, 2 * e + k, 0:HROW], attrT[:, h, j * P:(j + 1) * P], enc_b[:, :], start=True, stop=True)
                            ins.then_inc(a_encps, 1)
                            if q == 0:
                                pe.wait_ge(a_targets, i * 2 + (h + 1))
                            pe.wait_ge(a_prod, n + 1)
                            for k in range(2):
                                j = 2 * q + k
                                ins = pe.matmul(ps[:, 4 + 2 * e + k, 0:HROW], targets[h][:, j, :], hbuf[:, bass.ds(regs[j], 1), :].squeeze(1),
                                                start=True, stop=True)
                            ins.then_inc(a_hd, 1)

            def softmax(_):
                with pe.Fori(0, QM // BLK) as i:
                    pe.wait_ge(m_copied, i + 1)
                    pe.wait_ge(m_evac, i * 2 + 2)
                    for b in range(BLK):
                        pe.transpose(ps[:, 0, b * P:(b + 1) * P], work[:, b * P:(b + 1) * P], ident[:, :])
                        ins = pe.transpose(ps[:, 1, b * P:(b + 1) * P], work[:, 512 + b * P:512 + (b + 1) * P], ident[:, :])
                    ins.then_inc(m_turned, 1)
                one = ident[0:1, 0:1]
                for r in range(2):
                    pe.wait_ge(m_cols, 2 * r + 1)
                    for n in ((0, 1, 2, 3) if r == 0 else (3,)):
                        k = n if r == 0 else 0
                        ins = pe.transpose(ps[0:1, 0, k * P:(k + 1) * P], col[:, n:n + 1], ident[:, :])
                    ins.then_inc(m_row, 1)
                    pe.wait_ge(m_cols, 2 * r + 2)
                    for k, n in (((0, 4), (1, 5), (2, 7)) if r == 0 else ((0, 7),)):
                        ins = pe.transpose(ps[:, 1, k:k + 1], rowv(n, 1), one)
                    ins.then_inc(m_row, 1)
                with pe.Fori(0, QM // BLK) as i:
                    pe.wait_ge(m_exp, i + 1)
                    pe.wait_ge(m_out, i + 1)
                    for b in range(BLK):
                        ins = pe.transpose(ps[:, 2, b * P:(b + 1) * P], work[:, b * P:(b + 1) * P], ident[:, :])
                    ins.then_inc(m_back, 1)

            def gather_sum(_):
                pe.sem_inc(b_done, U)
                with pe.Fori(0, ITERS) as i:
                    for h in range(2):
                        for j in range(G):
                            s = i * U + (h * G + j)
                            if j == 0:
                                pe.wait_ge(b_mult, i * 2 + (h + 1))
                            pe.wait_ge(b_onehot, s + 1)
                            pe.wait_ge(b_added, s + 1)
                            pe.matmul(ps[:, j, 0:GROW], onehot[:, j, :], ring[:, h * G + j, :], start=True, stop=True).then_inc(b_done, 1)

            run(pe, {"setup": setup, "pass": products, "walk": walk, "heads": heads, "gat_rows": gat_rows_,
                     "scores": scores, "softmax": softmax, "gather_sum": gather_sum})


def kernel(**inputs):
    import numpy as np
    import concourse.bacc as bacc
    from concourse.bass_utils import run_bass_kernel_spmd

    v = {k: np.asarray(a) for k, a in inputs.items()}
    E, N = v["dst"].shape[0], v["x"].shape[0]
    tiles = -(-E // P)
    pad = tiles * P - E

    def edge_rows(a, fill=0):
        return np.pad(np.ascontiguousarray(a), (0, pad), constant_values=fill).view(np.int32).reshape(tiles, 1, P)

    attr = v["edge_attr_3"]
    edges = np.concatenate(
        [edge_rows(v["dst"], 1 << 14), edge_rows(v["src"]), edge_rows(v["edge_type_32"]), edge_rows(v["edge_type_16"]),
         edge_rows(v["edge_type_20"]), edge_rows(v["edge_weight1"][:, 0])] + [edge_rows(attr[:, c]) for c in range(3)], axis=1)
    windows = -(-N // (2 * P)) * 2
    arrays = {
        "x": np.pad(v["x"], ((0, windows * P - N), (0, 0))), "edges": edges,
        "dst_last": np.ascontiguousarray(edges[:, 0, P - 1]), "bases": v["L0_gnn_bases"],
        "w_compT": np.ascontiguousarray(v["L0_gnn_w_comp"].T), "w1": v["L1_gnn_weight"],
        "gate1T": np.ascontiguousarray(v["L1_gnn_gate_weight"][:, :, 0].T), "w2": v["L2_gnn_W"],
        "w2T": np.ascontiguousarray(v["L2_gnn_W"].T), "a_src": v["L2_gnn_a_src"], "a_dst": v["L2_gnn_a_dst"],
        "edge_wT": np.ascontiguousarray(v["L2_gnn_edge_W"].T), "edge_b": v["L2_gnn_edge_b"], "bias2": v["L2_gnn_bias"],
        "w3": v["L3_gnn_weight"], "ident_one": np.ones((1, HEADS, 1), np.float32),
    }
    nc = bacc.Bacc("TRN2", target_bir_lowering=False, num_devices=1)
    args = {k: nc.dram_tensor("in_" + k, a.shape, mybir.dt.from_np(a.dtype), kind="ExternalInput").ap() for k, a in arrays.items()}
    out = nc.dram_tensor("out_0", (N, D), F32, kind="ExternalOutput").ap()
    build(nc, out=out, **args)
    r = run_bass_kernel_spmd(nc, [{"in_" + k: np.ascontiguousarray(a) for k, a in arrays.items()}], core_ids=[0])
    return r.results[0]["out_0"]
```

```python
from contextlib import ExitStack

import concourse.bass as bass
from concourse import mybir

F32 = mybir.dt.float32
F32R = mybir.dt.float32r
I32 = mybir.dt.int32
U8 = mybir.dt.uint8
BF16 = mybir.dt.bfloat16
ALU = mybir.AluOpType
ACT = mybir.ActivationFunctionType
AX = mybir.AxisListType

P = 128
D = 256
HEADS, HD = 8, 32
HROW = HEADS * (HD + 1)
GROW = HEADS + D
W2C = D + 2 * HEADS
BASES = 8
R0, R1, R3 = 32, 16, 20
BIG = 1.0e30
EPS = 1e-5
G = 8
U = 2 * G
RH = 4
RU = RH * G
FIELDS = 9
DST, SRC, T32, T16, T20, NORM, ATTR = range(7)


def build(nc, x, edges, dst_last, bases, w_compT, w1, gate1T, w2, w2T, a_src, a_dst, edge_wT,
          edge_b, bias2, w3, ident_one, out, stop=None):
    N = out.shape[0]
    NWIN = x.shape[0] // P
    NW1 = -(-N // P)
    TILES = edges.shape[0]
    STEPS = TILES + NW1 - 1
    KP = -(-STEPS // RU) * RU
    KC = -(-KP // P)
    ITERS = KP // U
    RITERS = KP // RU
    QS = P // HEADS
    QM = KP // QS
    NSC = KP * HEADS
    BLK = 4
    assert NWIN % 2 == 0 and KP + G <= KC * P and KP % QS == 0 and QM % BLK == 0 and KP < 256 * 4

    table = nc.dram_tensor("table", (NWIN * P, R0 * D), F32).ap()
    w0_dram = nc.dram_tensor("w0_dram", (R0, D, D), F32).ap()
    attr_dram = nc.dram_tensor("attr_dram", (KC * P, 9, P), BF16).ap()
    place_dram = nc.dram_tensor("place_dram", (KP // G + 1, G * P), BF16).ap()
    rows_dram = nc.dram_tensor("rows_dram", (KP // G, P, G * GROW), F32).ap()
    gat_table = nc.dram_tensor("gat_table", (NWIN * P, GROW), F32).ap()

    with ExitStack() as ctx:
        def sb(name, shape, dt=F32):
            return ctx.enter_context(nc.sbuf_tensor(name, shape, dt))

        def sb_both(name, shape):
            with nc.sbuf_tensor(name, shape, F32) as plain:
                pass
            return plain, sb(name + "_r", shape, F32R)

        def sem(name):
            return ctx.enter_context(nc.semaphore(name))

        X = sb("X", [P, NWIN, D])
        A = sb("A", [P, 2 * NSC + 16])
        W, W_r = sb_both("W", [P, 2 * NSC])
        dloc = sb("dloc", [P, KP + G])
        norm = sb("norm", [P, KP + G])
        srcf = sb("srcf", [P, KP])
        types = sb("types", [P, 3, KP], U8)
        idx = sb("idx", [P, KP + RU], I32)
        win = sb("win", [1, KP], U8)
        ring = sb("ring", [P, U, GROW])
        onehot = sb("onehot", [P, G, P])
        targets1 = sb("targets1", [P, G * P])
        enc = A[:, NSC + 64:NSC + 64 + 4 * HROW].rearrange("p (n e c) -> p n e c", n=2, e=2)
        prod = A[:, NSC + 1280:NSC + 1280 + 4 * HROW].rearrange("p (n e c) -> p n e c", n=2, e=2)
        work, work_r = sb_both("work", [P, 2048])
        ident = sb("ident", [P, P])
        iota = sb("iota", [P, P])
        ix = sb("ix", [P, RH, G], I32)
        stat = sb("stat", [P, 4, NWIN])
        enc_w = sb("enc_w", [96, HROW])
        enc_b = sb("enc_b", [96, HROW], BF16)
        S = sb("S", [P, G, HEADS])
        small = sb("small", [P, 32])
        gate = sb("gate", [P, 2, R1])
        col = sb("col", [P, 8])
        ps = ctx.enter_context(nc.psum_tensor("ps", [P, 8, 512], F32))

        acc = A[:, 0:NWIN * GROW].rearrange("p (w c) -> p w c", c=GROW)
        UNIT = 3 * 512
        WHALF = 12 * 2 * D
        stage = A[:, 0:4 * UNIT].rearrange("p (s c) -> p s c", s=4)
        row_stats = work[:, 0:6 * NWIN].rearrange("p (w s) -> p w s", s=6)
        gates = A[:, 2 * NSC - NWIN * R1:2 * NSC].rearrange("p (w r) -> p w r", r=R1)
        xs = work[:, 0:512].rearrange("p (u c) -> p u c", u=2)
        xt = work[:, 512:1024].rearrange("p (u c n) -> p u c n", u=2, c=2)
        xt_high = work_r[:, 512:1024].rearrange("p (u c n) -> p u c n", u=2, c=2)
        xt_low = work_r[:, 1024:1536].rearrange("p (u c n) -> p u c n", u=2, c=2)
        attrT = work[0:96, 0:1024].bitcast(BF16).rearrange("p (h c) -> p h c", h=2)
        place = work[:, 1024:2048].bitcast(BF16).rearrange("p (h c) -> p h c", h=2)

        def w_rel(rels, low):
            return W_r[:, low * WHALF:low * WHALF + 2 * rels * D].rearrange("p (c n) -> p c n", c=2)

        alpha = A[:, 0:NSC].rearrange("p (k h) -> p k h", h=HEADS)
        hbuf = W[:, 0:NWIN * HROW].rearrange("p (w c) -> p w c", c=HROW)
        w2ext = work[:, 1024:1024 + 2 * W2C].rearrange("p (c o) -> p c o", c=2)
        gate_w = work[:, 1536:1536 + 2 * R1].rearrange("p (c r) -> p c r", c=2)
        gat_stage = A[:, 0:2 * W2C].rearrange("p (u c) -> p u c", u=2)
        w2nat = onehot[:, 0:4, :].rearrange("p (c a) b -> p c (a b)", c=2)
        gat_rows = gat_table.rearrange("(w p) c -> w p c", p=P)

        def row_halves(more):
            m = more.rearrange("p (s c) -> p s c", c=GROW)
            return [ring[:, 0:G, :], ring[:, G:U, :], m[:, 0:G, :], m[:, G:U, :]]

        score_rows = row_halves(A[:, 2 * NSC - U * GROW:2 * NSC])
        sum_rows = row_halves(W[:, 0:U * GROW])
        assert NSC + 1280 + 4 * HROW <= 2 * NSC - U * GROW and U * GROW <= NSC

        alphaT = W[:, 0:NSC]
        keyT = W[:, NSC:2 * NSC]
        maxT = W[:, NSC:2 * NSC]
        penalty = A[:, 0:NSC + 1]
        prefix = A[:, NSC + 8:2 * NSC + 8]
        ex = W[:, NSC:2 * NSC].rearrange("p (k h) -> p k h", h=HEADS)

        span = KC * P
        dl_i = A[0:NW1, 0:TILES].bitcast(I32)
        dl_f = A[0:NW1, 800:800 + TILES]
        k_i = A[0:NW1, 1600:1600 + span].bitcast(I32)
        k_f = A[0:NW1, 2500:2500 + span]
        below = A[0:NW1, 3400:3400 + span]
        junk = A[0:NW1, 4300:4300 + TILES]
        recf = A[:, 5200:5200 + KC * 5 * P].rearrange("p (k f e) -> p k f e", k=KC, f=5)
        parts = A[:, 0:KC * 9 * P // 2].bitcast(BF16).rearrange("p (k j f e) -> p k j f e", k=KC, j=3, f=3)
        rows16 = A[:, 4100:4100 + KC * P // 2].bitcast(BF16).rearrange("p (k e) -> p k e", k=KC)
        rows32 = A[:, 9700:9700 + KC * P].rearrange("p (k e) -> p k e", k=KC)
        wB = A[:, 12300:12300 + KP]
        rec = W[:, 0:KC * FIELDS * P].rearrange("p (k f e) -> p k f e", k=KC, f=FIELDS)
        w128_i = small[0:NW1, 0:1].bitcast(I32)
        w128_f = small[0:NW1, 1:2]
        below_count = small[0:NW1, 2:3]
        first_step = small[0:NW1, 3:4]
        ones_col = small[0:NW1, 16:17]
        ones_rows = onehot[0:NW1, 0, :]
        tile_f = stat[:, 0, 0:KC]
        step_f = stat[:, 1, 0:KC]
        step_i = stat[:, 2, 0:KC].bitcast(I32)
        tile_i = stat[:, 3, 0:KC].bitcast(I32)
        IB = D // 4
        HB = IB // 2
        Xflat = X[:, :, :].rearrange("p w c -> p (w c)")
        basesS = Xflat[0:4 * BASES, 0:HB * D]
        wout = Xflat[:, HB * D:HB * D + 4096].rearrange("p (s c) -> p s c", s=2)
        wsel = onehot[0:4 * BASES, 2, :]

        def rowv(n, m):
            return work[0:1, n * P:(n + m) * P]

        bar = sem("bar")
        dve_done = sem("dve_done")
        loaded = sem("loaded")
        stored = sem("stored")
        got = [sem(f"got{j}") for j in range(RU)]
        claimed = sem("claimed")
        u_iota, u_ident, u_below, u_win, u_tile, u_rec, u_recf, u_turned, u_evac, u_attr, u_wsel, u_wrow, u_half, u_wps, u_wevac = (
            sem("u_" + n) for n in ("iota", "ident", "below", "win", "tile", "rec", "recf", "turned",
                                    "evac", "attr", "wsel", "wrow", "half", "wps", "wevac"))
        u_parts, u_rows = sem("u_parts"), sem("u_rows")
        u_wst = [sem(f"u_wst{s}") for s in range(2)]
        ln_var, ln_std = sem("ln_var"), sem("ln_std")
        z_zero, z_ps, z_done, z_biased = sem("z_zero"), sem("z_ps"), sem("z_done"), sem("z_biased")
        ln_stats, ln_normed = sem("ln_stats"), sem("ln_normed")

        q_names = ("copied", "turned", "xt_high", "xt_ready", "bank_full", "bank_free", "unit_full", "gate_full", "gate_ready", "w_high")
        (q_copied, q_turned, q_xt_high, q_xt_ready, q_bank_full, q_bank_free, q_unit_full, q_gate_full, q_gate_ready,
         q_w_high) = (sem("q_" + n) for n in q_names)
        q_unit_free = [sem(f"q_unit_free{s}") for s in range(4)]
        q_w_low, q_gates_kept = sem("q_w_low"), sem("q_gates_kept")

        class Pass:
            def __init__(self, weights, rels, r0, total, gated, spare, ahead):
                self.weights, self.rels, self.r0, self.total, self.gated, self.ahead = weights, rels, r0, total, gated, ahead
                self.banks = rels * D // 512
                self.makes_gates = gated and not spare
                self.norms = {R1: 0, R3: 2}.get(total) if not spare else None
                self.unit_banks = [range(0, -(-self.banks // 2)), range(-(-self.banks // 2), self.banks)]
                assert not gated or 4 * UNIT + 2 * rels * D <= 2 * NSC - NWIN * R1
                assert len(self.unit_banks[0]) * 512 <= UNIT and 2 * rels * D <= WHALF and self.banks <= (4 if gated else 6)
                self.raw = (A[:, 4 * UNIT:4 * UNIT + 2 * rels * D].rearrange("p (c n) -> p c n", c=2)
                            if spare else W[:, WHALF:WHALF + 2 * rels * D].rearrange("p (c n) -> p c n", c=2))
                self.table = table.rearrange("n c -> (n c)")[0:NWIN * P * total * D]

        class Walk:
            def __init__(self, name, rounds, rels, tcol, table_):
                self.rounds, self.rels, self.tcol, self.table = rounds, rels, tcol, table_
                self.ix_free, self.ix_ready, self.onehot_ready, self.step_done, self.added = (
                    sem(f"{name}_{n}") for n in ("ix_free", "ix_ready", "onehot_ready", "step_done", "added"))

            def arrived(self, i, slot=0):
                return i * 16 + (16 + 16 * (self.rounds if slot < U else 0))

        def passes(weights, total, cuts, gated):
            made, r0 = [], total
            for n in reversed(range(len(cuts))):
                r0 -= cuts[n]
                made.insert(0, Pass(weights, cuts[n], r0, total, gated, n > 0, made[0] if made else None))
            assert r0 == 0
            return made

        p0 = passes(w0_dram, R0, (12, 10, 10), False)
        p1 = passes(w1, R1, (8, 8), True)
        p3 = passes(w3, R3, (10, 10), False)
        before = dict.fromkeys(q_names + ("unit_free",), 0)
        for p in p0 + p1 + p3:
            p.before = dict(before)
            for n, more in (("copied", NWIN), ("turned", NWIN), ("xt_high", NWIN), ("xt_ready", NWIN), ("w_high", p.banks),
                            ("bank_full", NWIN * p.banks), ("bank_free", (NWIN + 1) * p.banks), ("unit_full", 2 * NWIN),
                            ("gate_full", NWIN * p.makes_gates), ("gate_ready", (NWIN + 2) * p.gated),
                            ("unit_free", 16 * (NWIN // 2) + 16)):
                before[n] += more
        walk0 = Walk("s0", 0, R0, 0, p0[0].table)
        walk1 = Walk("s1", ITERS, R1, 1, p1[0].table)
        walk3 = Walk("s3", 2 * ITERS + RITERS, R3, 2, p3[0].table)
        gw = Walk("sg", 2 * ITERS, 1, 0, None)
        g_copied, g_turned, g_xt, g_out, g_row, g_hbuf = (sem("g_" + n) for n in (
            "copied", "turned", "xt", "out", "row", "hbuf"))
        g_stored = [sem(f"g_stored{u}") for u in range(2)]
        (a_targets, a_ones, a_encps, a_relu, a_hd, a_prod, a_red, a_alpha) = (
            sem("a_" + n) for n in ("targets", "ones", "encps", "relu", "hd", "prod", "red", "alpha"))
        a_attr = [sem(f"a_attr{h}") for h in range(2)]
        a_spill = [sem(f"a_spill{h}") for h in range(RH)]
        m_copied, m_turned, m_evac, m_exp, m_back, m_out, m_cols, m_row = (sem("m_" + n) for n in (
            "copied", "turned", "evac", "exp", "back", "out", "cols", "row"))
        b_row = [sem(f"b_row{h}") for h in range(RH)]
        b_exp, b_mult, b_onehot, b_done, b_added = (sem("b_" + n) for n in (
            "exp", "mult", "onehot", "done", "added"))

        def relational(ps_list, walk_):
            return [(part, p) for p in ps_list for part in ("split", "pass")] + [("walk", walk_)]

        PHASES = ([("setup", None), ("weights", p0[0])] + relational(p0, walk0) + [("norm", 0)] + relational(p1, walk1) +
                  [("norm", 1), ("heads", None), ("gat_rows", None), ("scores", None), ("softmax", None),
                   ("gather_sum", None), ("norm", 2)] + relational(p3, walk3) + [("norm", 3)])
        if stop is not None:
            PHASES = PHASES[:stop]

        def run(eng, parts):
            for n, (name, what) in enumerate(PHASES):
                if name in parts:
                    parts[name](what)
                eng.drain().then_inc(bar, 1)
                eng.wait_ge(bar, 5 * (n + 1))

        block = ctx.enter_context(nc.Block())

        @block.sync
        def _(sp):
            seen = [0]

            def load(dst, src):
                sp.dma_start(dst, src).then_inc(loaded, 16)
                seen[0] += 16

            def setup(_):
                load(dl_i, dst_last.partition_broadcast(NW1))
                sp.wait_ge(u_wsel, 1)
                for i4 in range(4):
                    sp.dma_start(wsel[i4 * BASES:(i4 + 1) * BASES, i4 * R0:(i4 + 1) * R0], w_compT).then_inc(u_wrow, 16)
                for half in range(2):
                    if half:
                        sp.wait_ge(u_wps, 16)
                    for i4 in range(4):
                        i0 = i4 * IB + half * HB
                        sp.dma_start(basesS[i4 * BASES:(i4 + 1) * BASES],
                                     bases[:, i0:i0 + HB, :].rearrange("b i o -> b (i o)")).then_inc(u_half, 16)
                    for n in range(4):
                        sp.wait_ge(u_wevac, 16 * half + 4 * n + 4)
                        for i4 in range(4):
                            i0 = i4 * IB + half * HB + n * 8
                            sp.dma_start(w0_dram[:, i0:i0 + 8, :].rearrange("r i o -> r (i o)"),
                                         wout[i4 * R0:(i4 + 1) * R0, n % 2, :]).then_inc(u_wst[n % 2], 16)
                for s in range(2):
                    sp.wait_ge(u_wst[s], 4 * 4 * 16)
                sp.wait_ge(u_parts, 1)
                for c in range(KC):
                    n = min(P, KP + G - c * P)
                    sp.dma_start(attr_dram[c * P:c * P + n].rearrange("k f e -> k (f e)"),
                                 parts[0:n, c].rearrange("p j f e -> p (j f e)")).then_inc(u_attr, 16)
                    sp.dma_start(place_dram.rearrange("g (k e) -> (g k) e", e=P)[c * P:c * P + n], rows16[0:n, c]).then_inc(u_attr, 16)
                load(X[:, :, :], x.rearrange("(w p) c -> p w c", p=P))
                sp.wait_ge(u_attr, 32 * KC)
                sp.wait_ge(loaded, seen[0])

            def load_raw(ps_):
                for c in range(2):
                    load(ps_.raw[:, c, :].rearrange("p (r o) -> p r o", o=D),
                         ps_.weights[ps_.r0:ps_.r0 + ps_.rels, c * P:(c + 1) * P, :].rearrange("r p o -> p r o"))
                if ps_.gated and ps_.r0 == 0:
                    load(gate_w[:, :, :], gate1T.rearrange("(c p) r -> p c r", p=P))

            def weights(ps_):
                load_raw(ps_)
                sp.wait_ge(loaded, seen[0])

            def store_table(ps_):
                if ps_.ahead is not None:
                    load_raw(ps_.ahead)
                rows = ps_.table.rearrange("(w p c) -> w p c", p=P, c=ps_.total * D)
                with sp.Fori(0, NWIN // 2) as i:
                    for u in range(2):
                        for v in range(2):
                            s, banks = 2 * u + v, ps_.unit_banks[v]
                            c0 = ps_.r0 * D + banks[0] * 512
                            sp.wait_ge(q_unit_full, i * 4 + (s + 1 + ps_.before["unit_full"]))
                            sp.dma_start(rows[bass.ds(i * 2 + u, 1), :, c0:c0 + len(banks) * 512].squeeze(0),
                                         stage[:, s, 0:len(banks) * 512]).then_inc(q_unit_free[s], 16)
                for s in range(4):
                    sp.wait_ge(q_unit_free[s], 16 * (NWIN // 2) + (16 + ps_.before["unit_free"]))
                sp.wait_ge(loaded, seen[0])

            def norm_loads(layer):
                if layer == 1:
                    for c in range(2):
                        load(w2ext[:, c, HEADS:HEADS + D], w2T[c * P:(c + 1) * P, :])
                        load(w2nat[:, c, :], w2[c * P:(c + 1) * P, :])
                    sp.wait_ge(z_zero, 1)
                    with nc.allow_non_contiguous_dma(reason="a few hundred words"):
                        for h in range(HEADS):
                            c, q = h // 4, h % 4
                            load(small[q * HD:(q + 1) * HD, 16 * c + h:16 * c + h + 1], a_src[h:h + 1, :].rearrange("a d -> d a"))
                            load(small[q * HD:(q + 1) * HD, 16 * c + 8 + h:16 * c + 9 + h], a_dst[h:h + 1, :].rearrange("a d -> d a"))
                        for j in range(3):
                            load(enc_w[32 * j + 9:32 * j + 10, :].rearrange("p (h d) -> p h d", d=HD + 1)[:, :, HD:HD + 1], ident_one)
                    for j in range(3):
                        for k in range(3):
                            load(enc_w[32 * j + 3 * k:32 * j + 3 * k + 3, :].rearrange("p (h d) -> p h d", d=HD + 1)[:, :, 0:HD],
                                 edge_wT.rearrange("k (h d) -> k h d", d=HD))
                        load(enc_w[32 * j + 9:32 * j + 10, :].rearrange("p (h d) -> p h d", d=HD + 1)[:, :, 0:HD],
                             edge_b.rearrange("(a h d) -> a h d", a=1, d=HD))
                sp.wait_ge(loaded, seen[0])
                if layer in (0, 2):
                    load_raw((p1 if layer == 0 else p3)[0])
                    sp.wait_ge(loaded, seen[0])

            def store_gat_rows(_):
                with sp.Fori(0, NWIN // 2) as i:
                    for u in range(2):
                        sp.wait_ge(g_row, i * 2 + (u + 3))
                        sp.dma_start(gat_rows[bass.ds(i * 2 + u, 1)].squeeze(0), gat_stage[:, u, 0:GROW]).then_inc(g_stored[u], 16)
                for u in range(2):
                    sp.wait_ge(g_stored[u], 16 * (NWIN // 2) + 16)

            def spill(_):
                sp.wait_ge(a_ones, 1)
                def attributes(i, h):
                    for j in range(3):
                        sp.dma_start(attrT[32 * j:32 * j + 9, h % 2, :].rearrange("c (k e) -> c k e", e=P),
                                     attr_dram[bass.ds(i * RU + h * G, G)].rearrange("k c e -> c k e")).then_inc(a_attr[h % 2], 16)
                    sp.dma_start(place[:, h % 2, :], place_dram[bass.ds(i * RH + h, 1)].squeeze(0).partition_broadcast(P)).then_inc(a_attr[h % 2], 16)

                attributes(0, 0)
                with sp.Fori(0, RITERS) as i:
                    for h in range(RH):
                        sp.wait_ge(a_hd, i * (2 * G) + ((h + 1) * G // 2 + G // 2))
                        attributes(i, h + 1)
                        for j in range(G):
                            sp.wait_ge(got[h * G + j], gw.arrived(i, h * G))
                        sp.dma_start(rows_dram[bass.ds(i * RH + h, 1)].squeeze(0).rearrange("p (s c) -> p s c", c=GROW),
                                     score_rows[h]).then_inc(a_spill[h], 16)
                for h in range(RH):
                    sp.wait_ge(a_spill[h], 16 * RITERS + 16)

            def load_bias(_):
                load(ring[:, 0, 0:D], bias2.partition_broadcast(P))
                sp.wait_ge(loaded, seen[0])
                sp.sem_inc(z_done, 1)

            def reload(_):
                with sp.Fori(0, RITERS) as i:
                    for h in range(RH):
                        sp.wait_ge(b_done, i * RU + (h * G + G))
                        sp.dma_start(sum_rows[h], rows_dram[bass.ds(i * RH + h, 1)].squeeze(0).rearrange("p (s c) -> p s c", c=GROW)
                                     ).then_inc(b_row[h], 16)

            run(sp, {"setup": setup, "weights": weights, "pass": store_table, "norm": norm_loads,
                     "gat_rows": store_gat_rows, "scores": spill, "softmax": load_bias, "gather_sum": reload})
            full = N // P
            sp.dma_start(out[0:full * P, :].rearrange("(w p) c -> p w c", p=P), X[:, 0:full, :]).then_inc(stored, 16)
            sp.dma_start(out[full * P:N, :], X[0:N - full * P, full, :]).then_inc(stored, 16)
            sp.wait_ge(stored, 32)

        @block.gpsimd
        def _(pool):
            def setup(_):
                pool.iota(w128_i, [[0, 1]], base=0, channel_multiplier=P).then_inc(u_iota, 1)
                pool.iota(k_i, [[1, span]], base=0, channel_multiplier=0).then_inc(u_iota, 1)
                pool.iota(step_i, [[P, KC]], base=0, channel_multiplier=1).then_inc(u_iota, 1)
                pool.iota(iota[:, :], [[1, P]], base=0, channel_multiplier=0,
                          allow_small_or_imprecise_dtypes=True).then_inc(u_iota, 1)
                pool.iota(col[:, 7:8], [[0, 1]], base=0, channel_multiplier=1,
                          allow_small_or_imprecise_dtypes=True).then_inc(u_iota, 1)
                pool.memset(ident[:, :], 0.0).then_inc(u_ident, 1)
                pool.wait_ge(u_ident, 1)
                pool.affine_select(out=ident[:, :], in_=ident[:, :], compare_op=ALU.not_equal, fill=1.0,
                                   base=0, pattern=[[-1, P]], channel_multiplier=1).then_inc(u_ident, 1)
                pool.wait_ge(u_tile, 1)
                for c in range(KC):
                    pool.indirect_dma_start(out=rec[:, c, :, :].rearrange("p f e -> p (f e)").bitcast(I32), out_offset=None,
                                            in_=edges.rearrange("t f e -> t (f e)"),
                                            in_offset=bass.IndirectOffsetOnAxis(ap=tile_i[:, c:c + 1], axis=0)).then_inc(u_rec, 16)
                pool.wait_ge(u_rec, 16 * KC)

            def gather(src, places, wk, spilled=None):
                halves = len(places)
                with pool.Fori(0, KP // (halves * G)) as i:
                    for h, place_ in enumerate(places):
                        pool.wait_ge(wk.ix_ready, i * halves + (h + 1))
                        if spilled is not None:
                            pool.wait_ge(spilled[h], i * 16 + 16)
                        pool.sem_inc(claimed, 1)
                        for j in range(G):
                            pool.indirect_dma_start(out=place_[:, j, :], out_offset=None, in_=src,
                                                    in_offset=bass.IndirectOffsetOnAxis(ap=ix[:, h, j:j + 1], axis=0)
                                                    ).then_inc(got[h * G + j], 16)

            def walk(wk):
                gather(wk.table.rearrange("(a o) -> a o", o=D), [ring[:, h * G:(h + 1) * G, 0:D] for h in range(2)], wk)

            def scores(_):
                gather(gat_table, score_rows, gw, a_spill)

            def weigh(_):
                with pool.Fori(0, RITERS) as i:
                    for h, half in enumerate(sum_rows):
                        rows = half[:, :, HEADS:GROW].rearrange("p k (h d) -> p k h d", d=HD)
                        pool.wait_ge(b_exp, i * RH + (h + 1))
                        pool.tensor_tensor(rows, rows, half[:, :, 0:HEADS].unsqueeze(3).to_broadcast([P, G, HEADS, HD]),
                                           ALU.mult).then_inc(b_mult, 1)

            def add_bias(_):
                pool.wait_ge(z_done, 1)
                pool.tensor_tensor(X[:, :, :], X[:, :, :], ring[:, 0:1, 0:D].to_broadcast([P, NWIN, D]), ALU.add).then_inc(z_biased, 1)

            run(pool, {"setup": setup, "walk": walk, "scores": scores, "softmax": add_bias, "gather_sum": weigh})

        @block.vector
        def _(dve):
            done = [0]

            def ch(ins):
                ins.then_inc(dve_done, 1)
                done[0] += 1
                dve.wait_ge(dve_done, done[0])

            def setup(_):
                ch(dve.memset(wsel, 0.0))
                dve.sem_inc(u_wsel, 1)
                ch(dve.memset(ones_rows, 1.0))
                ch(dve.memset(ones_col, 1.0))
                dve.wait_ge(u_iota, 5)
                dve.wait_ge(loaded, 16)
                ch(dve.tensor_copy(dl_f, dl_i))
                ch(dve.tensor_copy(w128_f, w128_i))
                ch(dve.tensor_copy(k_f, k_i))
                ch(dve.tensor_scalar(junk, dl_f, w128_f, 0.0, ALU.is_lt, ALU.add, accum_out=below_count))
                ch(dve.scalar_tensor_tensor(first_step, w128_f, 1.0 / P, below_count, ALU.mult, ALU.add))
                ch(dve.tensor_scalar(below, k_f, first_step, None, ALU.is_ge))
                dve.sem_inc(u_below, 1)
                dve.wait_ge(u_win, 1)
                for c in range(2):
                    n = min(span // 2, KP - c * (span // 2))
                    ch(dve.tensor_scalar(wB[:, c * (span // 2):c * (span // 2) + n], ps[:, c, 0:n], -1.0, None, ALU.add))
                ch(dve.tensor_copy(win[0:1, :], wB[0:1, :]))
                ch(dve.tensor_copy(step_f, step_i))
                ch(dve.scalar_tensor_tensor(tile_f, ps[:, 2, 0:KC], -1.0, step_f, ALU.mult, ALU.add))
                ch(dve.tensor_scalar(tile_i, tile_f, 1.0, float(TILES - 1), ALU.add, ALU.min))
                dve.sem_inc(u_tile, 1)
                dve.wait_ge(u_rec, 16 * KC)
                ch(dve.tensor_copy(recf, rec[:, :, 0:5, :].bitcast(I32)))
                dve.sem_inc(u_recf, 1)
                dest = [dloc, srcf, types[:, 0, :], types[:, 1, :], types[:, 2, :], norm]
                for f in range(6):
                    for c in range(KC):
                        m, n = f * KC + c, min(P, KP - c * P)
                        dve.wait_ge(u_turned, m + 1)
                        dve.tensor_copy(dest[f][:, c * P:c * P + n], ps[:, 3 + m % 3, 0:n]).then_inc(u_evac, 1)
                dve.wait_ge(u_evac, 6 * KC)
                attrs = rec[:, :, ATTR:ATTR + 3, :]
                for n in range(3):
                    ch(dve.tensor_copy(parts[:, :, n], attrs))
                    if n < 2:
                        ch(dve.tensor_tensor(attrs, attrs, parts[:, :, n], ALU.subtract))
                ch(dve.tensor_scalar(tile_f, ps[:, 2, 0:KC], -1.0, float(P), ALU.add, ALU.mult))
                for c in range(KC):
                    dve.tensor_scalar(rows32[:, c], recf[:, c, DST, :], tile_f[:, c:c + 1], -1.0, ALU.subtract, ALU.max).then_inc(u_rows, 1)
                dve.wait_ge(u_rows, KC)
                ch(dve.tensor_scalar(rows16, rows32, float(P), None, ALU.min))
                dve.sem_inc(u_parts, 1)
                ch(dve.scalar_tensor_tensor(dloc[:, 0:KP], wB, -float(P), dloc[:, 0:KP], ALU.mult, ALU.add))
                ch(dve.memset(dloc[:, STEPS:KP + G], -1.0))
                ch(dve.memset(norm[:, KP:KP + G], 0.0))
                ch(dve.memset(idx[:, KP:KP + RU], 0.0))

            def split(ps_):
                for b in range(ps_.banks):
                    bank = slice(b * 512, (b + 1) * 512)
                    low = w_rel(ps_.rels, 1)[:, :, bank]
                    dve.wait_ge(q_w_high, b + (1 + ps_.before["w_high"]))
                    dve.tensor_tensor(low, ps_.raw[:, :, bank], w_rel(ps_.rels, 0)[:, :, bank].bitcast(F32), ALU.subtract).then_inc(q_w_low, 1)

            def copies(ps_):
                def to_place(window, u):
                    if ps_.norms is not None:
                        normalise(window, xs[:, u, :], q_copied)
                        normalise(window)
                    else:
                        dve.tensor_copy(xs[:, u, :], X[:, bass.ds(window, 1), :].squeeze(1)).then_inc(q_copied, 1)

                def body(i, more):
                    for u in range(2):
                        turned = ps[:, 6 + u, 0:D].rearrange("p (c n) -> p c n", c=2)
                        dve.wait_ge(q_turned, i * 2 + (u + 1 + ps_.before["turned"]))
                        dve.tensor_copy(xt_high[:, u, :, :], turned).then_inc(q_xt_high, 1)
                        if more:
                            to_place(i * 2 + (u + 2), u)
                        dve.wait_ge(q_xt_high, i * 2 + (u + 1 + ps_.before["xt_high"]))
                        dve.tensor_tensor(xt_low[:, u, :, :], turned, xt_high[:, u, :, :].bitcast(F32), ALU.subtract).then_inc(q_xt_ready, 1)

                for u in range(2):
                    to_place(u, u)
                with dve.Fori(0, NWIN // 2 - 1) as i:
                    body(i, True)
                body(NWIN // 2 - 1, False)

            def window_registers(i, h):
                _, regs = nc.values_load_multi_w_load_instructions(
                    win[0:1, bass.ds(i * U + h * G, G)], engines=[dve.engine], min_val=0, max_val=NWIN - 1,
                    skip_runtime_bounds_check_because="a step's window counts windows that have begun, at most all of them")
                return regs

            def steps(width, weighed, onehot_ready, step_done, added, granted=U):
                def build(s, j):
                    dve.tensor_scalar(onehot[:, j, :], iota[:, :], dloc[:, s], norm[:, s] if weighed else None, ALU.is_equal,
                                      ALU.mult if weighed else ALU.bypass).then_inc(onehot_ready, 1)

                for j in range(G):
                    build(slice(j, j + 1), j)
                with dve.Fori(0, ITERS) as i:
                    for h in range(2):
                        regs = window_registers(i, h)
                        for j in range(G):
                            dve.wait_ge(step_done, i * U + (h * G + j + 1 + granted))
                            build(bass.ds(i * U + (h * G + j + G), 1), j)
                            dve.wait_ge(added, i * U + (h * G + j + G))
                            a = acc[:, bass.ds(regs[j], 1), 0:width].squeeze(1)
                            dve.tensor_tensor(a, a, ps[:, j, 0:width], ALU.add).then_inc(added, 1)
                dve.wait_ge(added, KP + G)
                dve.wait_ge(onehot_ready, KP + G)

            def walk(wk):
                ch(dve.scalar_tensor_tensor(idx[:, 0:KP], srcf[:, :], float(wk.rels), types[:, wk.tcol, :], ALU.mult, ALU.add))
                ch(dve.memset(A[:, 0:NWIN * GROW], 0.0))
                dve.sem_inc(wk.ix_free, 1)
                dve.sem_inc(wk.added, G)
                steps(D, True, wk.onehot_ready, wk.step_done, wk.added)

            def normalise(window, to=None, done_=ln_normed):
                row = X[:, bass.ds(window, 1), :].squeeze(1)
                dve.tensor_scalar(row if to is None else to, row, stat[:, 0, bass.ds(window, 1)],
                                  stat[:, 2, bass.ds(window, 1)], ALU.subtract, ALU.mult).then_inc(done_, 1)

            def residual_norm(layer):
                mean, var, rstd = stat[:, 0, :], stat[:, 1, :], stat[:, 2, :]
                if layer == 1:
                    ch(dve.memset(small[:, :], 0.0))
                    ch(dve.memset(enc_w[:, :], 0.0))
                    dve.sem_inc(z_zero, 1)
                if layer == 2:
                    a = acc[:, :, HEADS:GROW]
                    ch(dve.tensor_scalar(acc[:, :, 0:HEADS], acc[:, :, 0:HEADS], 1e-10, None, ALU.max))
                    ch(dve.reciprocal(acc[:, :, 0:HEADS], acc[:, :, 0:HEADS]))
                    ah = a.rearrange("p w (h d) -> p w h d", d=HD)
                    ch(dve.tensor_tensor(ah, ah, acc[:, :, 0:HEADS].unsqueeze(3).to_broadcast([P, NWIN, HEADS, HD]), ALU.mult))
                    ch(dve.tensor_tensor(X[:, :, :], a, X[:, :, :], ALU.add))
                else:
                    ch(dve.scalar_tensor_tensor(X[:, :, :], acc[:, :, 0:D], 0.0, X[:, :, :], ALU.max, ALU.add))
                with dve.Fori(0, NWIN // 2) as i:
                    for u in range(2):
                        dve.bn_stats(row_stats[:, bass.ds(i * 2 + u, 1), :].squeeze(1),
                                     X[:, bass.ds(i * 2 + u, 1), :].squeeze(1)).then_inc(ln_stats, 1)
                dve.wait_ge(ln_stats, NWIN * (layer + 1))
                mean_e, dev_e, mean_o, dev_o = (row_stats[:, :, n] for n in (1, 2, 4, 5))
                ch(dve.tensor_tensor(mean, mean_e, mean_o, ALU.add))
                ch(dve.tensor_scalar(mean, mean, 0.5, None, ALU.mult))
                ch(dve.tensor_tensor(rstd, mean_e, mean_o, ALU.subtract))
                ch(dve.tensor_tensor(rstd, rstd, rstd, ALU.mult))
                ch(dve.tensor_tensor(var, dev_e, dev_o, ALU.add))
                ch(dve.scalar_tensor_tensor(var, rstd, D / 4.0, var, ALU.mult, ALU.add))
                ch(dve.tensor_scalar(var, var, 1.0 / D, EPS, ALU.mult, ALU.add))
                dve.sem_inc(ln_var, 1)
                dve.wait_ge(ln_std, layer + 1)
                ch(dve.reciprocal(rstd, rstd))
                if layer in (1, 3):
                    with dve.Fori(0, NWIN // 2) as i:
                        for u in range(2):
                            normalise(i * 2 + u)
                    dve.wait_ge(ln_normed, NWIN * (layer + 1))

            def heads(_):
                part, rest = A[0:96, 0:HROW // 2].bitcast(BF16), A[0:96, 512:512 + HROW]
                ch(dve.tensor_copy(part, enc_w[:, :]))
                ch(dve.tensor_copy(enc_b[0:32, :], part[0:32]))
                ch(dve.tensor_tensor(rest, enc_w[:, :], part, ALU.subtract))
                ch(dve.tensor_copy(part, rest))
                ch(dve.tensor_copy(enc_b[32:64, :], part[32:64]))
                ch(dve.tensor_tensor(rest, rest, part, ALU.subtract))
                ch(dve.tensor_copy(enc_b[64:96, :], rest[64:96]))
                for c in range(2):
                    dve.wait_ge(z_ps, c + 1)
                    ch(dve.tensor_copy(w2ext[:, c, 0:HEADS], ps[:, c, 0:HEADS]))
                    ch(dve.tensor_copy(w2ext[:, c, HEADS + D:W2C], ps[:, c, HEADS:2 * HEADS]))

            def gat_rows_(_):
                dve.sem_inc(g_hbuf, 2)
                with dve.Fori(0, NWIN // 2) as i:
                    for u in range(2):
                        dve.tensor_copy(xs[:, u, :], X[:, bass.ds(i * 2 + u, 1), :].squeeze(1)).then_inc(g_copied, 1)
                    for u in range(2):
                        dve.wait_ge(g_turned, i * 2 + (u + 1))
                        dve.tensor_copy(xt[:, u, :, :], ps[:, 6 + u, 0:D].rearrange("p (c n) -> p c n", c=2)).then_inc(g_xt, 1)
                    for u in range(2):
                        dve.wait_ge(g_row, i * 2 + (u + 3))
                        row = hbuf[:, bass.ds(i * 2 + u, 1), :].squeeze(1).rearrange("p (h d) -> p h d", d=HD + 1)
                        dve.tensor_copy(row[:, :, 0:HD], gat_stage[:, u, HEADS:HEADS + D].rearrange("p (h d) -> p h d", d=HD))
                        dve.tensor_copy(row[:, :, HD:HD + 1], gat_stage[:, u, HEADS + D:W2C].unsqueeze(2)).then_inc(g_hbuf, 1)

            def scores(_):
                ch(dve.tensor_copy(idx[:, 0:KP], srcf[:, :]))
                for h in range(RH):
                    dve.tensor_copy(ix[:, h, :], idx[:, h * G:(h + 1) * G]).then_inc(gw.ix_ready, 1)
                ch(dve.memset(attrT[:, :, :], 0.0))
                for j in range(3):
                    ch(dve.memset(attrT[32 * j:32 * j + 10, :, :], 1.0))
                dve.sem_inc(a_ones, 1)
                dve.sem_inc(a_prod, 2)
                dve.sem_inc(a_red, 2)
                dve.sem_inc(a_alpha, 1)
                targets = [onehot[:, :, :].rearrange("p k e -> p (k e)"), targets1[:, :]]

                def target_matrices(i, h):
                    dve.wait_ge(a_attr[h % 2], i * (64 * RH // 2) + (h // 2 * 64 + 64))
                    dve.tensor_scalar(targets[h % 2], place[:, h % 2, :], col[:, 7:8], None, ALU.is_equal).then_inc(a_targets, 1)

                target_matrices(0, 0)
                with dve.Fori(0, RITERS) as i:
                    for h in range(RH):
                        def reduce_pair(n, q):
                            dve.wait_ge(a_prod, n + 3)
                            if q == 0:
                                dve.wait_ge(a_alpha, i * RH + (h + 1))
                            dve.tensor_reduce(S[:, 2 * q:2 * q + 2, :], prod[:, q % 2].rearrange("p e (h d) -> p e h d", d=HD + 1),
                                              AX.X, ALU.add).then_inc(a_red, 1)

                        for q in range(4):
                            n = i * (2 * G) + (h * 4 + q)
                            dve.wait_ge(a_hd, n + (1 + G))
                            dve.wait_ge(a_relu, n + 3)
                            dve.wait_ge(a_red, n + 1)
                            dve.tensor_tensor(prod[:, q % 2], enc[:, q % 2], ps[:, 4 + 2 * (q % 2):6 + 2 * (q % 2), 0:HROW],
                                              ALU.mult).then_inc(a_prod, 1)
                            if q == 1:
                                target_matrices(i, h + 1)
                            if q:
                                reduce_pair(i * (2 * G) + (h * 4 + q - 1), q - 1)
                        reduce_pair(i * (2 * G) + (h * 4 + 3), 3)
                        dve.wait_ge(a_red, i * (2 * G) + (h * 4 + 4 + 2))
                        for j in range(G):
                            dve.wait_ge(got[h * G + j], gw.arrived(i, h * G))
                        dve.tensor_tensor(alpha[:, bass.ds(i * RU + h * G, G), :], S[:, :, :],
                                          score_rows[h][:, :, 0:HEADS], ALU.add).then_inc(a_alpha, 1)
                        dve.wait_ge(a_alpha, i * RH + (h + 2))
                        dve.tensor_copy(ix[:, h, :], idx[:, bass.ds(i * RU + (h * G + RU), G)]).then_inc(gw.ix_ready, 1)
                dve.wait_ge(gw.ix_ready, RH * RITERS + RH)

            def softmax(_):
                ch(dve.scalar_tensor_tensor(A[:, 0:NSC], A[:, 0:NSC], 0.2, A[:, 0:NSC], ALU.mult, ALU.max))
                dve.sem_inc(m_turned, 1)
                av = A[:, 0:NSC].rearrange("p (q m h) -> p q m h", q=QS, h=HEADS)
                dv = dloc[:, 0:KP].rearrange("p (q m) -> p q m", q=QS)
                with dve.Fori(0, QM // BLK) as i:
                    dve.wait_ge(m_turned, i + 1)
                    for b in range(BLK):
                        dst = work[:, b * P:(b + 1) * P].rearrange("p (q h) -> p q h", h=HEADS)
                        key = work[:, 512 + b * P:512 + (b + 1) * P].rearrange("p (q h) -> p q h", h=HEADS)
                        dve.tensor_copy(dst, av[:, :, bass.ds(i * BLK + b, 1), :].squeeze(2))
                        ins = dve.tensor_copy(key, dv[:, :, bass.ds(i * BLK + b, 1)].to_broadcast([P, QS, HEADS]))
                    ins.then_inc(m_copied, 1)
                dve.wait_ge(m_evac, 2 * (QM // BLK) + 2)
                ch(dve.tensor_tensor(penalty[:, 1:NSC], keyT[:, 1:NSC], keyT[:, 0:NSC - 1], ALU.not_equal))
                ch(dve.tensor_scalar(penalty[:, 1:NSC], penalty[:, 1:NSC], -BIG, None, ALU.mult))
                ch(dve.tensor_reduce(col[:, 0:1], penalty[:, 1:NSC], AX.X, ALU.min))
                ch(dve.tensor_copy(col[:, 1:2], keyT[:, 0:1]))
                ch(dve.tensor_copy(col[:, 2:3], keyT[:, NSC - 1:NSC]))
                ch(dve.memset(penalty[:, 0:1], -BIG))
                ch(dve.tensor_tensor_scan(prefix, penalty[:, 0:NSC], alphaT, -BIG, ALU.add, ALU.max))
                ch(dve.tensor_copy(col[:, 3:4], prefix[:, NSC - 1:NSC]))
                dve.sem_inc(m_cols, 1)
                dve.wait_ge(m_row, 1)
                ch(dve.tensor_copy(rowv(0, 4), ps[0:1, 0, 0:4 * P]))
                whole, fk, lk, tail, link, nlink, pen_q, car = (rowv(n, 1) for n in range(8))
                H8 = HEADS
                ch(dve.memset(link, 0.0))
                ch(dve.tensor_tensor(link[:, H8:P], fk[:, H8:P], lk[:, 0:P - H8], ALU.is_equal))
                ch(dve.tensor_scalar(link, link, -1.0, BIG, ALU.add, ALU.mult))
                ch(dve.memset(nlink, -BIG))
                ch(dve.tensor_copy(nlink[:, 0:P - H8], link[:, H8:P]))
                by_head = "o (q h) -> o h q"
                a_hq, b_hq, c_hq = (rowv(n, 1) for n in (8, 9, 10))
                hq = "o (h q) -> o h q"

                def carries(lnk, ends, rev, out_row):
                    ch(dve.tensor_tensor(pen_q, lnk, whole, ALU.add))
                    for src_, dst_ in ((pen_q, a_hq), (ends, b_hq)):
                        v = src_.rearrange(by_head, h=HEADS)
                        v = v[:, :, ::-1] if rev else v
                        ch(dve.tensor_copy(dst_.rearrange(hq, h=HEADS), v))
                    ch(dve.tensor_tensor_scan(c_hq, a_hq, b_hq, -BIG, ALU.add, ALU.max))
                    ch(dve.memset(out_row, -BIG))
                    o = out_row.rearrange(by_head, h=HEADS)
                    cv = c_hq.rearrange(hq, h=HEADS)
                    if rev:
                        ch(dve.tensor_copy(o[:, :, 0:QS - 1], cv[:, :, 0:QS - 1][:, :, ::-1]))
                    else:
                        ch(dve.tensor_copy(o[:, :, 1:QS], cv[:, :, 0:QS - 1]))

                carries(link, tail, False, car)
                dve.sem_inc(m_cols, 1)
                dve.wait_ge(m_row, 2)
                ch(dve.tensor_copy(col[:, 4:7], ps[:, 1, 0:3]))
                ch(dve.tensor_copy(penalty[:, 0:1], col[:, 4:5]))
                ch(dve.tensor_copy(penalty[:, NSC:NSC + 1], col[:, 5:6]))
                ch(dve.tensor_tensor_scan(prefix, penalty[:, 0:NSC], alphaT, col[:, 6:7], ALU.add, ALU.max))
                ch(dve.tensor_tensor_scan(maxT[:, ::-1], penalty[:, 1:NSC + 1][:, ::-1], prefix[:, ::-1], -BIG, ALU.add, ALU.max))
                ch(dve.tensor_copy(col[:, 3:4], maxT[:, 0:1]))
                dve.sem_inc(m_cols, 1)
                dve.wait_ge(m_row, 3)
                ch(dve.tensor_copy(tail, ps[0:1, 0, 0:P]))
                carries(nlink, tail, True, car)
                dve.sem_inc(m_cols, 1)
                dve.wait_ge(m_row, 4)
                ch(dve.tensor_copy(col[:, 6:7], ps[:, 1, 0:1]))
                ch(dve.tensor_tensor_scan(maxT[:, ::-1], penalty[:, 1:NSC + 1][:, ::-1], prefix[:, ::-1], col[:, 6:7], ALU.add, ALU.max))
                ch(dve.tensor_tensor(alphaT, alphaT, maxT, ALU.subtract))
                dve.sem_inc(m_back, 1)
                dve.sem_inc(m_out, 1)
                exq = W[:, NSC:2 * NSC].rearrange("p (q m h) -> p q m h", q=QS, h=HEADS)
                with dve.Fori(0, QM // BLK) as i:
                    dve.wait_ge(m_back, i + 2)
                    for b in range(BLK):
                        ins = dve.tensor_copy(exq[:, :, bass.ds(i * BLK + b, 1), :].squeeze(2),
                                              ps[:, 2, b * P:(b + 1) * P].rearrange("p (q h) -> p q h", h=HEADS))
                    ins.then_inc(m_out, 1)
                ch(dve.memset(A[:, 0:NWIN * GROW], 0.0))

            def gather_sum(_):
                dve.sem_inc(b_added, G)
                steps(GROW, False, b_onehot, b_done, b_added, RU)

            run(dve, {"setup": setup, "split": split, "pass": copies, "walk": walk, "norm": residual_norm, "heads": heads,
                      "gat_rows": gat_rows_, "scores": scores, "softmax": softmax, "gather_sum": gather_sum})

        @block.scalar
        def _(act):
            def setup(_):
                for m in range(32):
                    n = m // 4
                    act.wait_ge(u_wps, m + 1)
                    if m % 4 == 0 and n >= 2:
                        act.wait_ge(u_wst[n % 2], 64 * (n // 2))
                    act.activation(wout[:, n % 2, (m % 4) * 512:(m % 4 + 1) * 512], ps[:, 6 + m % 2, :], ACT.Copy).then_inc(u_wevac, 1)

            def split(ps_):
                for b in range(ps_.banks):
                    bank = slice(b * 512, (b + 1) * 512)
                    act.activation(w_rel(ps_.rels, 0)[:, :, bank], ps_.raw[:, :, bank], ACT.Copy).then_inc(q_w_high, 1)

            def evacuate(ps_):
                act.sem_inc(q_bank_free, ps_.banks)
                if ps_.gated:
                    act.sem_inc(q_gate_ready, 2)
                for s in range(4):
                    act.sem_inc(q_unit_free[s], 16)
                with act.Fori(0, NWIN // 2) as i:
                    for u in range(2):
                        if ps_.gated:
                            of_window = gates[:, bass.ds(i * 2 + u, 1), :].squeeze(1)
                            if ps_.makes_gates:
                                act.wait_ge(q_gate_full, i * 2 + (u + 1 + ps_.before["gate_full"]))
                                act.activation(gate[:, u, :], ps[:, 4 + u, 0:R1], ACT.Sigmoid).then_inc(q_gate_ready, 1)
                            else:
                                act.activation(gate[:, u, :], of_window, ACT.Copy).then_inc(q_gate_ready, 1)
                            act.wait_ge(q_gate_ready, i * 2 + (u + 3 + ps_.before["gate_ready"]))
                        for v in range(2):
                            s = 2 * u + v
                            act.wait_ge(q_unit_free[s], i * 16 + (16 + ps_.before["unit_free"]))
                            for k, b in enumerate(ps_.unit_banks[v]):
                                dst = stage[:, s, k * 512:(k + 1) * 512]
                                act.wait_ge(q_bank_full, i * (2 * ps_.banks) + (u * ps_.banks + b + 1 + ps_.before["bank_full"]))
                                if ps_.gated:
                                    r = ps_.r0 + 2 * b
                                    act.activation(dst[:, 0:D], ps[:, b, 0:D], ACT.Copy, scale=gate[:, u, r:r + 1])
                                    ins = act.activation(dst[:, D:512], ps[:, b, D:512], ACT.Copy, scale=gate[:, u, r + 1:r + 2])
                                else:
                                    ins = act.activation(dst, ps[:, b, :], ACT.Copy)
                                ins.then_inc(q_bank_free, 1)
                            act.wait_ge(q_bank_free, i * (2 * ps_.banks) + ((u + 1) * ps_.banks + ps_.unit_banks[v][-1] + 1 + ps_.before["bank_free"]))
                            act.sem_inc(q_unit_full, 1)
                        if ps_.makes_gates:
                            act.activation(of_window, gate[:, u, :], ACT.Copy).then_inc(q_gates_kept, 1)

            def indices(wk):
                act.wait_ge(wk.ix_free, 1)
                with act.Fori(0, ITERS) as i:
                    for h in range(2):
                        act.wait_ge(wk.step_done, i * U + (h * G + G))
                        act.activation(ix[:, h, :], idx[:, bass.ds(i * U + h * G, G)], ACT.Copy).then_inc(wk.ix_ready, 1)

            def std(layer):
                act.wait_ge(ln_var, layer + 1)
                act.activation(stat[:, 2, :], stat[:, 1, :], ACT.Sqrt).then_inc(ln_std, 1)

            def gat_rows_(_):
                act.sem_inc(g_row, 2)
                for u in range(2):
                    act.sem_inc(g_stored[u], 16)
                with act.Fori(0, NWIN // 2) as i:
                    for u in range(2):
                        act.wait_ge(g_out, i * 2 + (u + 1))
                        act.wait_ge(g_stored[u], i * 16 + 16)
                        act.wait_ge(g_hbuf, i * 2 + (u + 1))
                        act.activation(gat_stage[:, u, :], ps[:, u, 0:W2C], ACT.Copy).then_inc(g_row, 1)

            def scores(_):
                act.sem_inc(a_relu, 2)
                for h in range(RH):
                    act.sem_inc(a_spill[h], 16)
                with act.Fori(0, ITERS) as i:
                    for q in range(G):
                        n, e = i * G + q, q % 2
                        act.wait_ge(a_encps, n + 1)
                        act.wait_ge(a_prod, n + 1)
                        act.activation(enc[:, e], ps[:, 2 * e:2 * e + 2, 0:HROW], ACT.Relu).then_inc(a_relu, 1)

            def softmax(_):
                act.sem_inc(m_evac, 2)
                with act.Fori(0, QM // BLK) as i:
                    act.wait_ge(m_turned, i + 2)
                    act.activation(W[:, bass.ds(i * 512, 512)], ps[:, 0, :], ACT.Copy).then_inc(m_evac, 1)
                    act.activation(W[:, bass.ds(i * 512 + NSC, 512)], ps[:, 1, :], ACT.Copy).then_inc(m_evac, 1)
                with act.Fori(0, QM // BLK) as i:
                    act.wait_ge(m_back, i + 1)
                    act.activation(work[:, 0:512], W[:, bass.ds(i * 512, 512)], ACT.Exp).then_inc(m_exp, 1)

            def exps(_):
                with act.Fori(0, RITERS) as i:
                    for h in range(RH):
                        act.wait_ge(b_row[h], i * 16 + 16)
                        act.activation(sum_rows[h][:, :, 0:HEADS], ex[:, bass.ds(i * RU + h * G, G), :], ACT.Copy).then_inc(b_exp, 1)

            run(act, {"setup": setup, "split": split, "pass": evacuate, "walk": indices, "norm": std, "gat_rows": gat_rows_,
                      "scores": scores, "softmax": softmax, "gather_sum": exps})

        @block.tensor
        def _(pe):
            def setup(_):
                pe.wait_ge(u_below, 1)
                for c in range(2):
                    pe.matmul(ps[:, c, 0:span // 2], ones_rows, below[:, c * (span // 2):(c + 1) * (span // 2)], start=True, stop=True)
                for c in range(KC):
                    ins = pe.matmul(ps[:, 2, c:c + 1], below[:, c * P:(c + 1) * P], ones_col, start=True, stop=True)
                ins.then_inc(u_win, 1)
                pe.wait_ge(u_wrow, 64)
                for m in range(32):
                    if m % 16 == 0:
                        pe.wait_ge(u_half, 64 * (m // 16 + 1))
                    if m >= 2:
                        pe.wait_ge(u_wevac, m - 1)
                    pe.matmul(ps[:, 6 + m % 2, :], wsel, basesS[:, (m % 16) * 512:(m % 16 + 1) * 512], start=True, stop=True).then_inc(u_wps, 1)
                pe.wait_ge(u_recf, 1)
                pe.wait_ge(u_ident, 2)
                for f in range(6):
                    for c in range(KC):
                        m = f * KC + c
                        if m >= 3:
                            pe.wait_ge(u_evac, m - 2)
                        pe.transpose(ps[:, 3 + m % 3, 0:P], recf[:, c, f, :] if f < 5 else rec[:, c, NORM, :], ident[:, :]).then_inc(u_turned, 1)

            def turn(i, copied, turned_):
                for u in range(2):
                    pe.wait_ge(copied, i * 2 + (u + 1))
                    for c in range(2):
                        ins = pe.transpose(ps[:, 6 + u, c * P:(c + 1) * P], xs[:, u, c * P:(c + 1) * P], ident[:, :])
                    ins.then_inc(turned_, 1)

            def products(ps_):
                high, low = w_rel(ps_.rels, 0), w_rel(ps_.rels, 1)

                def turn_window(n, u):
                    pe.wait_ge(q_copied, n + (1 + ps_.before["copied"]))
                    for c in range(2):
                        ins = pe.transpose(ps[:, 6 + u, c * P:(c + 1) * P], xs[:, u, c * P:(c + 1) * P], ident[:, :])
                    ins.then_inc(q_turned, 1)

                def body(i, more):
                    for u in range(2):
                        pe.wait_ge(q_xt_ready, i * 2 + (u + 1 + ps_.before["xt_ready"]))
                        if ps_.makes_gates:
                            pe.wait_ge(q_gate_ready, i * 2 + (u + 1 + ps_.before["gate_ready"]))
                            for n in range(4):
                                ins = pe.matmul(ps[:, 4 + u, 0:R1], (xt_high, xt_low)[n // 2][:, u, n % 2, :].bitcast(F32), gate_w[:, n % 2, :],
                                                start=(n == 0), stop=(n == 3))
                            ins.then_inc(q_gate_full, 1)
                        for b in range(ps_.banks):
                            pe.wait_ge(q_bank_free, i * (2 * ps_.banks) + (u * ps_.banks + b + 1 + ps_.before["bank_free"]))
                            terms = [(xt_high, high, c) for c in range(2)] + [(xt_high, low, c) for c in range(2)] + [(xt_low, high, c) for c in range(2)]
                            for n, (rows, w, c) in enumerate(terms):
                                ins = pe.matmul(ps[:, b, :], rows[:, u, c, :], w[:, c, b * 512:(b + 1) * 512],
                                                start=(n == 0), stop=(n == len(terms) - 1))
                            ins.then_inc(q_bank_full, 1)
                        if more:
                            turn_window(i * 2 + (u + 2), u)

                for u in range(2):
                    turn_window(u, u)
                with pe.Fori(0, NWIN // 2 - 1) as i:
                    body(i, True)
                body(NWIN // 2 - 1, False)

            def walk(wk):
                pe.sem_inc(wk.step_done, U)
                with pe.Fori(0, ITERS) as i:
                    for h in range(2):
                        for j in range(G):
                            s = i * U + (h * G + j)
                            pe.wait_ge(got[h * G + j], wk.arrived(i))
                            pe.wait_ge(wk.onehot_ready, s + 1)
                            pe.wait_ge(wk.added, s + 1)
                            pe.matmul(ps[:, j, 0:D], onehot[:, j, :], ring[:, h * G + j, 0:D], start=True, stop=True).then_inc(wk.step_done, 1)

            def heads(_):
                for c in range(2):
                    for k in range(2):
                        ins = pe.matmul(ps[:, c, 0:2 * HEADS], w2nat[:, k, c * P:(c + 1) * P], small[:, 16 * k:16 * k + 16],
                                        start=(k == 0), stop=(k == 1))
                    ins.then_inc(z_ps, 1)

            def gat_rows_(_):
                with pe.Fori(0, NWIN // 2) as i:
                    turn(i, g_copied, g_turned)
                    for u in range(2):
                        pe.wait_ge(g_xt, i * 2 + (u + 1))
                        pe.wait_ge(g_row, i * 2 + (u + 1))
                        for c in range(2):
                            ins = pe.matmul(ps[:, u, 0:W2C], xt[:, u, c, :], w2ext[:, c, :], start=(c == 0), stop=(c == 1))
                        ins.then_inc(g_out, 1)

            def scores(_):
                pe.sem_inc(a_hd, G)
                targets = [onehot, targets1[:, :].rearrange("p (k e) -> p k e", e=P)]
                with pe.Fori(0, RITERS) as i:
                    for h in range(RH):
                        _, regs = nc.values_load_multi_w_load_instructions(
                            win[0:1, bass.ds(i * RU + h * G, G)], engines=[pe.engine], min_val=0, max_val=NWIN - 1,
                            skip_runtime_bounds_check_because="a step's window counts windows that have begun, at most all of them")
                        pe.wait_ge(a_attr[h % 2], i * (64 * RH // 2) + (h // 2 * 64 + 64))
                        for q in range(4):
                            n, e = i * (2 * G) + (h * 4 + q), q % 2
                            pe.wait_ge(a_relu, n + 1)
                            for k in range(2):
                                j = 2 * q + k
                                ins = pe.matmul(ps[:, 2 * e + k, 0:HROW], attrT[:, h % 2, j * P:(j + 1) * P], enc_b[:, :], start=True, stop=True)
                            ins.then_inc(a_encps, 1)
                            if q == 0:
                                pe.wait_ge(a_targets, i * RH + (h + 1))
                            pe.wait_ge(a_prod, n + 1)
                            for k in range(2):
                                j = 2 * q + k
                                ins = pe.matmul(ps[:, 4 + 2 * e + k, 0:HROW], targets[h % 2][:, j, :], hbuf[:, bass.ds(regs[j], 1), :].squeeze(1),
                                                start=True, stop=True)
                            ins.then_inc(a_hd, 1)

            def softmax(_):
                with pe.Fori(0, QM // BLK) as i:
                    pe.wait_ge(m_copied, i + 1)
                    pe.wait_ge(m_evac, i * 2 + 2)
                    for b in range(BLK):
                        pe.transpose(ps[:, 0, b * P:(b + 1) * P], work[:, b * P:(b + 1) * P], ident[:, :])
                        ins = pe.transpose(ps[:, 1, b * P:(b + 1) * P], work[:, 512 + b * P:512 + (b + 1) * P], ident[:, :])
                    ins.then_inc(m_turned, 1)
                one = ident[0:1, 0:1]
                for r in range(2):
                    pe.wait_ge(m_cols, 2 * r + 1)
                    for n in ((0, 1, 2, 3) if r == 0 else (3,)):
                        k = n if r == 0 else 0
                        ins = pe.transpose(ps[0:1, 0, k * P:(k + 1) * P], col[:, n:n + 1], ident[:, :])
                    ins.then_inc(m_row, 1)
                    pe.wait_ge(m_cols, 2 * r + 2)
                    for k, n in (((0, 4), (1, 5), (2, 7)) if r == 0 else ((0, 7),)):
                        ins = pe.transpose(ps[:, 1, k:k + 1], rowv(n, 1), one)
                    ins.then_inc(m_row, 1)
                with pe.Fori(0, QM // BLK) as i:
                    pe.wait_ge(m_exp, i + 1)
                    pe.wait_ge(m_out, i + 1)
                    for b in range(BLK):
                        ins = pe.transpose(ps[:, 2, b * P:(b + 1) * P], work[:, b * P:(b + 1) * P], ident[:, :])
                    ins.then_inc(m_back, 1)

            def gather_sum(_):
                pe.sem_inc(b_done, RU)
                with pe.Fori(0, RITERS) as i:
                    for h in range(RH):
                        pe.wait_ge(b_mult, i * RH + (h + 1))
                        for j in range(G):
                            s = i * RU + (h * G + j)
                            pe.wait_ge(b_onehot, s + 1)
                            pe.wait_ge(b_added, s + 1)
                            pe.matmul(ps[:, j, 0:GROW], onehot[:, j, :], sum_rows[h][:, j, :], start=True, stop=True).then_inc(b_done, 1)

            run(pe, {"setup": setup, "pass": products, "walk": walk, "heads": heads, "gat_rows": gat_rows_,
                     "scores": scores, "softmax": softmax, "gather_sum": gather_sum})


def kernel(**inputs):
    import numpy as np
    import concourse.bacc as bacc
    from concourse.bass_utils import run_bass_kernel_spmd

    v = {k: np.asarray(a) for k, a in inputs.items()}
    E, N = v["dst"].shape[0], v["x"].shape[0]
    tiles = -(-E // P)
    pad = tiles * P - E

    def edge_rows(a, fill=0):
        return np.pad(np.ascontiguousarray(a), (0, pad), constant_values=fill).view(np.int32).reshape(tiles, 1, P)

    attr = v["edge_attr_3"]
    edges = np.concatenate(
        [edge_rows(v["dst"], 1 << 14), edge_rows(v["src"]), edge_rows(v["edge_type_32"]), edge_rows(v["edge_type_16"]),
         edge_rows(v["edge_type_20"]), edge_rows(v["edge_weight1"][:, 0])] + [edge_rows(attr[:, c]) for c in range(3)], axis=1)
    windows = -(-N // (2 * P)) * 2
    arrays = {
        "x": np.pad(v["x"], ((0, windows * P - N), (0, 0))), "edges": edges,
        "dst_last": np.ascontiguousarray(edges[:, 0, P - 1]), "bases": v["L0_gnn_bases"],
        "w_compT": np.ascontiguousarray(v["L0_gnn_w_comp"].T), "w1": v["L1_gnn_weight"],
        "gate1T": np.ascontiguousarray(v["L1_gnn_gate_weight"][:, :, 0].T), "w2": v["L2_gnn_W"],
        "w2T": np.ascontiguousarray(v["L2_gnn_W"].T), "a_src": v["L2_gnn_a_src"], "a_dst": v["L2_gnn_a_dst"],
        "edge_wT": np.ascontiguousarray(v["L2_gnn_edge_W"].T), "edge_b": v["L2_gnn_edge_b"], "bias2": v["L2_gnn_bias"],
        "w3": v["L3_gnn_weight"], "ident_one": np.ones((1, HEADS, 1), np.float32),
    }
    nc = bacc.Bacc("TRN2", target_bir_lowering=False, num_devices=1)
    args = {k: nc.dram_tensor("in_" + k, a.shape, mybir.dt.from_np(a.dtype), kind="ExternalInput").ap() for k, a in arrays.items()}
    out = nc.dram_tensor("out_0", (N, D), F32, kind="ExternalOutput").ap()
    build(nc, out=out, **args)
    r = run_bass_kernel_spmd(nc, [{"in_" + k: np.ascontiguousarray(a) for k, a in arrays.items()}], core_ids=[0])
    return r.results[0]["out_0"]
```
